# Optimizing a Trainium2 kernel written in Bass

```python
import numpy as np
import jax
import jax.numpy as jnp

def _softmax(x, axis=-1):
    return jax.nn.softmax(x, axis=axis)

def _gelu(x):
    return jax.nn.gelu(x, approximate=True)

def _silu(x):
    return jax.nn.silu(x)

def _sigmoid(x):
    return jax.nn.sigmoid(x)

def _layernorm(x, axis=-1, eps=1e-05):
    m = jnp.mean(x, axis=axis, keepdims=True)
    v = jnp.var(x, axis=axis, keepdims=True)
    return (x - m) / jnp.sqrt(v + eps)

def _scatter_add(tgt, idx, src, axis=0):
    return tgt.at[idx].add(src)

def _segment_sum(src, seg, n):
    return jax.ops.segment_sum(src, seg, n)
kernel_name = 'mk_xattn_ffn_d1_seqx_r4_ddef49'

def setup_inputs(seed: int=0):
    np.random.seed(seed)
    _w = jnp.asarray

    def _rec_inputs():
        import jax
        import jax.numpy as jnp
        _rk = jax.random.key(seed)
        x = 0.5 + 0.2887 * jax.random.normal(jax.random.fold_in(_rk, 1), (4, 512, 512), jnp.float32)
        _lenS = 512 - jax.random.randint(jax.random.fold_in(_rk, 7), (4,), 0, max(1, 512 // 4) + 1, jnp.int32)
        _lenS2 = 512 - jax.random.randint(jax.random.fold_in(_rk, 8), (4,), 0, max(1, 512 // 4) + 1, jnp.int32)
        _ctx_512P = jax.random.normal(jax.random.fold_in(_rk, 11), (4, 16, 128), jnp.float32)
        _ctx_512c = jax.random.dirichlet(jax.random.fold_in(_rk, 511), 0.3 * jnp.ones((16,), jnp.float32), (4, 512))
        _ctx_512t = jnp.einsum('bsk,bkd->bsd', _ctx_512c, _ctx_512P)
        _ctx_512t = _ctx_512t * jax.lax.rsqrt(jnp.mean(jnp.square(_ctx_512t)) + 1e-12) * 0.953939
        ctx_512 = 7.22013e-05 + 1.00017 * (_ctx_512t + 0.3 * jax.random.normal(jax.random.fold_in(_rk, 611), (4, 512, 128), jnp.float32))
        _validS = jnp.arange(512)[None, :] < _lenS[:, None]
        _validS2 = jnp.arange(512)[None, :] < _lenS2[:, None]
        _causal = jnp.tril(jnp.ones((512, 512), dtype=bool))
        mask_SxS2_bk1 = jnp.broadcast_to(_validS2[0:1, :], (512, 512))
        mask_BxS2_bf0 = jnp.logical_not(jnp.ones((4, 512), dtype=bool))
        return (x, ctx_512, mask_SxS2_bk1, mask_BxS2_bf0)
    x, ctx_512, mask_SxS2_bk1, mask_BxS2_bf0 = _rec_inputs()

    def _L0_xattn_setup():
        import jax, jax.numpy as jnp
        import numpy as np
        B, S, H = (8, 512, 128)
        key = jax.random.key(seed)
        kq, kk, kqc, kwq, kwk = jax.random.split(key, 5)
        q = jax.random.normal(kq, (B, S, H), dtype=jnp.float32)
        k = jax.random.normal(kk, (B, S, H), dtype=jnp.float32)
        qc_score = jax.random.uniform(kqc, (B, S, S), dtype=jnp.float32)
        attn_mask = jnp.triu(jnp.ones((S, S), dtype=bool), k=1)
        key_padding_mask = jnp.zeros((B, S), dtype=bool)
        scale = 1.0 / np.sqrt(H)
        Wq = jax.random.normal(kwq, (H, H), dtype=jnp.float32) * scale
        Wk = jax.random.normal(kwk, (H, H), dtype=jnp.float32) * scale
        bq = jnp.zeros((H,), dtype=jnp.float32)
        bk = jnp.zeros((H,), dtype=jnp.float32)
        return {'q': q, 'k': k, 'attn_mask': attn_mask, 'key_padding_mask': key_padding_mask, 'qc_score': qc_score, 'Wq': Wq, 'bq': bq, 'Wk': Wk, 'bk': bk}
    _L0_xattn_all = _L0_xattn_setup()
    _L0_xattn_in = {k: v for k, v in _L0_xattn_all.items() if k in ('Wq', 'bq', 'Wk', 'bk')}
    del _L0_xattn_all

    def _L0_ffn_setup():
        import jax, jax.numpy as jnp
        import numpy as np
        B, S, D, I, E, K = (4, 256, 512, 256, 8, 2)
        key = jax.random.key(seed)
        ks = jax.random.split(key, 7)

        def w(k, shape, fan_in):
            return jax.random.normal(k, shape, dtype=jnp.float32) * fan_in ** (-0.5)
        return {'hidden_states': jax.random.normal(ks[0], (B, S, D), dtype=jnp.float32), 'router_w': w(ks[1], (D, E), D), 'gate_up_w': w(ks[2], (E, D, 2 * I), D), 'down_w': w(ks[3], (E, I, D), I), 'shared_gate_w': w(ks[4], (D, I), D), 'shared_up_w': w(ks[5], (D, I), D), 'shared_down_w': w(ks[6], (I, D), I)}
    _L0_ffn_all = _L0_ffn_setup()
    _L0_ffn_in = {k: v for k, v in _L0_ffn_all.items() if k in ('router_w', 'gate_up_w', 'down_w', 'shared_gate_w', 'shared_up_w', 'shared_down_w')}
    del _L0_ffn_all
    return {'x': x, 'ctx_512': ctx_512, 'mask_SxS2_bk1': mask_SxS2_bk1, 'mask_BxS2_bf0': mask_BxS2_bf0, 'L0_xattn_Wq': _L0_xattn_in['Wq'], 'L0_xattn_bq': _L0_xattn_in['bq'], 'L0_xattn_Wk': _L0_xattn_in['Wk'], 'L0_xattn_bk': _L0_xattn_in['bk'], 'L0_ffn_router_w': _L0_ffn_in['router_w'], 'L0_ffn_gate_up_w': _L0_ffn_in['gate_up_w'], 'L0_ffn_down_w': _L0_ffn_in['down_w'], 'L0_ffn_shared_gate_w': _L0_ffn_in['shared_gate_w'], 'L0_ffn_shared_up_w': _L0_ffn_in['shared_up_w'], 'L0_ffn_shared_down_w': _L0_ffn_in['shared_down_w']}

def reference(x, ctx_512, mask_SxS2_bk1, mask_BxS2_bf0, L0_xattn_Wq, L0_xattn_bq, L0_xattn_Wk, L0_xattn_bk, L0_ffn_router_w, L0_ffn_gate_up_w, L0_ffn_down_w, L0_ffn_shared_gate_w, L0_ffn_shared_up_w, L0_ffn_shared_down_w):
    import jax
    import jax.numpy as jnp

    def _L0_xattn_ref(q, k, attn_mask, key_padding_mask, qc_score, Wq, bq, Wk, bk):
        import jax, jax.numpy as jnp
        import numpy as np
        B, S, H = (8, 512, 128)
        qp = jnp.einsum('bsh,oh->bso', q, Wq) + bq
        kp = jnp.einsum('bth,oh->bto', k, Wk) + bk
        scaling = jnp.asarray(float(H) ** (-0.5), dtype=qp.dtype)
        scores = jnp.einsum('bsh,bth->bst', qp, kp) * scaling
        scores = scores * qc_score
        mask = attn_mask[None, :, :] | key_padding_mask[:, None, :]
        scores = jnp.where(mask, -jnp.inf, scores)
        return jax.nn.softmax(scores, axis=-1)

    def _L0_ffn_ref(hidden_states, router_w, gate_up_w, down_w, shared_gate_w, shared_up_w, shared_down_w):
        import jax, jax.numpy as jnp
        import numpy as np
        B, S, D, I, E, K = (4, 256, 512, 256, 8, 2)
        Bb, Ss, Dd = hidden_states.shape
        x = hidden_states.reshape(-1, Dd)
        T = x.shape[0]
        shared = jax.nn.silu(x @ shared_gate_w) * (x @ shared_up_w) @ shared_down_w
        logits = x @ router_w
        top_val, top_idx = jax.lax.top_k(logits, K)
        probs = jnp.zeros_like(logits).at[jnp.arange(T)[:, None], top_idx].set(jax.nn.sigmoid(top_val))
        xin = probs.T[:, :, None] * x[None]
        gu = jnp.einsum('etd,edf->etf', xin, gate_up_w)
        gate, up = jnp.split(gu, 2, axis=-1)
        h = jax.nn.silu(gate) * up
        expert_out = jnp.einsum('eti,eid->etd', h, down_w)
        combined = shared + expert_out.sum(axis=0)
        return combined.reshape(Bb, Ss, Dd)
    x = x + _L0_xattn_ref(ctx_512, ctx_512, mask_SxS2_bk1, mask_BxS2_bf0, _layernorm(x, axis=-1), L0_xattn_Wq, L0_xattn_bq, L0_xattn_Wk, L0_xattn_bk)
    x = x + _L0_ffn_ref(_layernorm(x, axis=-1), L0_ffn_router_w, L0_ffn_gate_up_w, L0_ffn_down_w, L0_ffn_shared_gate_w, L0_ffn_shared_up_w, L0_ffn_shared_down_w)
    return x

_drawn_inputs = setup_inputs


def setup_inputs(seed=0):
    import zlib

    import numpy as np

    out = dict(_drawn_inputs(seed))
    spreads = {'L0_xattn_bq': (0.0, 0.1), 'L0_xattn_bk': (0.0, 0.1)}
    factors = {}
    for name, (base, spread) in spreads.items():
        noise = np.random.default_rng([zlib.crc32(name.encode()), seed]).standard_normal(out[name].shape)
        drawn = base * np.exp(spread * noise) if base else spread * noise
        out[name] = jnp.asarray(drawn.astype(out[name].dtype))
    for name, factor in factors.items():
        out[name] = (out[name] * factor).astype(out[name].dtype)
    return out
```

```python
import numpy as np
import concourse.bass as bass
from concourse import mybir
from contextlib import ExitStack

P = 128
B, S, D, H = 4, 512, 512, 128
T = B * S
TILES = T // P
RT = S // P
KC = D // P
E, K, I = 8, 2, 256
IC = I // P
SHARED = E
ROUTED = (K * T + E * (P - 1)) // P
JOBS = TILES + ROUTED
EPS = 1e-5
SCALING = float(H) ** -0.5
BIG = 3e38
MASKED = -1e30
LAG = 2
HEAD = RT + LAG
LOOP_END = B - 1
SLOTS = 4


def build(nc, x, ctx, mask, kpad, wq, bq, wk, bk, router_w, gate_up_w, down_w, sg_w, su_w, sd_w, out):
    f32, bf16, i32, u8 = mybir.dt.float32, mybir.dt.bfloat16, mybir.dt.int32, mybir.dt.uint8
    ALU, ACT, X = mybir.AluOpType, mybir.ActivationFunctionType, mybir.AxisListType.X

    x_t = x.rearrange("b (r p) d -> (b r) p d", p=P)
    out_t = out.rearrange("(t p) d -> t p d", p=P)
    xn_dram = nc.dram_tensor("xn_rows", (T, D), f32, kind="Internal").ap()
    xn_t = xn_dram.rearrange("(t p) d -> t p d", p=P)

    stack = ExitStack()
    with stack:
        def sb(name, shape, dt=f32):
            return stack.enter_context(nc.sbuf_tensor(name, shape, dt))

        def sem(name):
            return stack.enter_context(nc.semaphore(name))

        def sems(name, n=SLOTS):
            return [sem(f"{name}{i}") for i in range(n)]

        gu = sb("gu", [P, E + 1, KC, 2 * I])
        dn = sb("dn", [P, E + 1, IC, D])
        rw = sb("rw", [P, KC, E])
        wqk = sb("wqk", [P, 2, H])
        wqkT = sb("wqkT", [P, 2, H])
        bqk = sb("bqk", [P, 2])
        ident = sb("ident", [P, P])
        ones = sb("ones", [P, P])
        triangle = sb("triangle", [P, P])
        ctx_all = sb("ctx_all", [P, TILES * H + 2 * S])
        ctx_in = ctx_all[:, 0:TILES * H].rearrange("p (t h) -> p t h", h=H)
        ctxT = ctx_all[:, TILES * H:].rearrange("p (a s) -> p a s", a=2)
        qkT = sb("qkT", [P, 2 * T])
        qT = qkT[:, 0:T]
        kT = qkT[:, T:2 * T]
        q_tile = sb("q_tile", [P, SLOTS, P])
        mask_in = sb("mask_in", [P, RT, S], u8)
        kpad_in = sb("kpad_in", [P, B, S], u8)
        pens = sb("pens", [P, RT + B + SLOTS, S], bf16)
        mask_pen = pens[:, 0:RT]
        kpad_pen = pens[:, RT:RT + B]
        pen = pens[:, RT + B:]
        xin = sb("xin", [P, SLOTS, D])
        sc = sb("sc", [P, SLOTS, S])
        x2 = sb("x2", [P, SLOTS, D])
        xn = sb("xn", [P, SLOTS, D])
        bn1 = sb("bn1", [P, SLOTS, 6])
        mv1 = sb("mv1", [P, SLOTS, 2])
        bn2 = sb("bn2", [P, SLOTS, 6])
        mv2 = sb("mv2", [P, SLOTS, 2])
        ve1 = sb("ve1", [P, SLOTS])
        ve2 = sb("ve2", [P, SLOTS])
        rstd1 = sb("rstd1", [P, SLOTS])
        rstd2 = sb("rstd2", [P, SLOTS])
        rowmax = sb("rowmax", [P, SLOTS])
        nbias = sb("nbias", [P, SLOTS])
        rowsum = sb("rowsum", [P, SLOTS])
        rsraw = sb("rsraw", [P, SLOTS])
        rinv = sb("rinv", [P, SLOTS])
        mhalf = sb("mhalf", [P, 1])
        xg = sc
        xT = sb("xT", [P, 2, KC, P])
        sg = sb("sg", [P, 2, I])
        h = sb("h", [P, 2, I])
        hT = sb("hT", [P, 2, IC, P])
        y = xin
        jprob = sb("jprob", [P, JOBS])
        jexpert = sb("jexpert", [P, JOBS], i32)
        jgather = sb("jgather", [P, ROUTED], i32)
        jscatter = sb("jscatter", [P, ROUTED], i32)
        gidx = sb("gidx", [P, SLOTS, 1], i32)
        sidx = sb("sidx", [P, SLOTS, 1], i32)
        NG = ROUTED + 1
        spare = [0]

        def old(name_, shape):
            n = int(np.prod(shape[1:]))
            at, spare[0] = spare[0], spare[0] + n
            letters = "abc"[:len(shape) - 1]
            return pens[:].rearrange("p r s -> p (r s)").bitcast(f32)[:, at:at + n].rearrange(
                f"p ({' '.join(letters)}) -> p {' '.join(letters)}", **dict(zip(letters[1:], shape[2:])))

        G = old("G", [P, K * TILES, NG])
        lg = sb("lg", [P, TILES, E])
        eq = old("eq", [P, TILES, E])
        key = old("key", [P, TILES, E])
        lg2 = old("lg2", [P, TILES, E])
        oh = sb("oh", [P, K, TILES, E])
        ohs = sb("ohs", [P, TILES, E])
        top = sb("top", [P, K, TILES])
        best = sb("best", [P, TILES])
        prob = sb("prob", [P, K, TILES])
        pexp = sb("pexp", [P, K, TILES])
        idx8 = old("idx8", [P, TILES, E])
        rank = old("rank", [P, 2, TILES, E])
        cum = old("cum", [P, 2, TILES, E])
        cnt = sb("cnt", [P, E])
        k128 = old("k128", [P, E, TILES])
        cmp = old("cmp", [P, E, TILES])
        ntile = sb("ntile", [P, 4, E])
        place = old("place", [P, TILES, E])
        slot1 = sb("slot1", [P, K, TILES])
        base = sb("base", [P, E])
        a128 = sb("a128", [P, NG])
        R = ctx_all[:, 0:K * TILES * 2 * ROUTED].rearrange("p (c m a) -> p c m a", m=2, a=ROUTED)
        acol = sb("acol", [P, K * TILES])
        bcol = sb("bcol", [P, K * TILES])
        tok1 = sb("tok1", [P, K, TILES])
        iota1 = sb("iota1", [P, P])
        OB = qkT[:].rearrange("p (c j) -> p c j", j=P)
        ecmp = sb("ecmp", [P, ROUTED, E])
        efl = sb("efl", [P, ROUTED])
        amap = sb("amap", [P, 2, ROUTED])
        pidx = sb("pidx", [P, 1])
        hole = sb("hole", [P, ROUTED])
        jf = sb("jf", [P, ROUTED])

        bank = [stack.enter_context(nc.psum_tensor(f"bank{i}", [P, 512], f32)) for i in range(8)]
        ps_score = bank[0:2]
        ps_xnT = bank[2:4]
        ps_logit = bank[4]
        ps_ctxT = bank[7]
        ps_proj = bank[5:7]
        ps_g = bank[0:2]
        ps_xT = bank[2]
        ps_hT = bank[3]
        ps_y = bank[5:7]
        ps_rank = bank[4]
        ps_map = bank[7]

        ld_ctx, ld_small, ld_mask, ld_rw, ld_ws, ld_w = sem("ld_ctx"), sem("ld_small"), sem("ld_mask"), sem("ld_rw"), sem("ld_ws"), sem("ld_w")
        ld_x, st_x2, st_xn = sems("ld_x"), sems("st_x2"), sems("st_xn")
        ld_xg, ld_x2, st_y = sems("ld_xg"), sems("ld_x2"), sems("st_y")
        gt_xg, add_y = sems("gt_xg"), sems("add_y")
        st_trash = sem("st_trash")
        c_pool = sem("c_pool")
        c_zero = sem("c_zero")
        pen_ready0 = sem("pen_ready0")
        wT_ps, wT_ready, ctxT_ps, ctxT_ready, proj_ps, proj_ready = (
            sem("wT_ps"), sem("wT_ready"), sem("ctxT_ps"), sem("ctxT_ready"), sem("proj_ps"), sem("proj_ready"))
        bq_ready = sem("bq_ready")
        q_ready, score_ps, xstat, bn1_s, bn2_s, ve1_s, ve2_s = (
            sem("q_ready"), sem("score_ps"), sem("xstat"), sem("bn1_s"), sem("bn2_s"), sem("ve1_s"), sem("ve2_s"))
        rstd1_s, rstd2_s, pen_s, raw_s, max_s, nbias_s, exp_s, rinv_s, x2_s, mv2_s, xn_s = (
            sem("rstd1_s"), sem("rstd2_s"), sem("pen_s"), sem("raw_s"), sem("max_s"), sem("nbias_s"), sem("exp_s"),
            sem("rinv_s"), sem("x2_s"), sem("mv2_s"), sem("xn_s"))
        xnT_ps, xnT_ready, logit_ps = sem("xnT_ps"), sem("xnT_ready"), sem("logit_ps")
        jxT_ps, jxT_s, g_ps, silu_s, h_s, hT_ps, hT_s, y_ps, y_s = (
            sem("jxT_ps"), sem("jxT_s"), sem("g_ps"), sem("silu_s"), sem("h_s"), sem("hT_ps"), sem("hT_s"),
            sem("y_ps"), sem("y_s"))
        lg_s, top_s, pexp_s, oh_s, rank_ps, rank_s, map_ps, map_s, table_s = (
            sem("lg_s"), sem("top_s"), sem("pexp_s"), sem("oh_s"), sem("rank_ps"), sem("rank_s"),
            sem("map_ps"), sem("map_s"), sem("table_s"))
        consts_s, prob_s, G_s, R_s, OB_s = sem("consts_s"), sem("prob_s"), sem("G_s"), sem("R_s"), sem("OB_s")
        rsum_s, rsraw_s = sem("rsum_s"), sem("rsraw_s")
        gidx_s, sidx_s = sem("gidx_s"), sem("sidx_s")
        pool_step, dve_step = sem("pool_step"), sem("dve_step")
        first_table = sem("first_table")

        block = stack.enter_context(nc.Block())

        def shift(q, r, by):
            return q + (r + by) // SLOTS, (r + by) % SLOTS

        def before(engine, value):
            if not isinstance(value, int):
                value = engine.snap(engine.to_reg(value))
                engine.wait_ge(c_pool, 1)
            return value

        def num(q, r):
            return SLOTS * q + r

        J0 = TILES // SLOTS

        def early(q):
            return isinstance(q, int) and q < 0

        @block.sync
        def _(sp):
            sp.dma_start(wqk[:, 0, :], wq).then_inc(ld_small, 16)
            sp.dma_start(wqk[:, 1, :], wk).then_inc(ld_small, 16)
            sp.dma_start(bqk[:, 0:1], bq.rearrange("(p o) -> p o", o=1)).then_inc(ld_small, 16)
            sp.dma_start(bqk[:, 1:2], bk.rearrange("(p o) -> p o", o=1)).then_inc(ld_small, 16)
            sp.dma_start(ctx_in, ctx.rearrange("b (r p) h -> p (b r) h", p=P)).then_inc(ld_ctx, 16)
            for r in range(SLOTS):
                sp.dma_start(xin[:, r, :], x_t[r]).then_inc(ld_x[r], 16)
            sp.dma_start(rw[:], router_w.rearrange("(k p) e -> p k e", p=P)).then_inc(ld_rw, 16)
            sp.dma_start(gu[:, SHARED, :, 0:I], sg_w.rearrange("(k p) f -> p k f", p=P)).then_inc(ld_ws, 16)
            sp.dma_start(gu[:, SHARED, :, I:2 * I], su_w.rearrange("(k p) f -> p k f", p=P)).then_inc(ld_ws, 16)
            sp.dma_start(dn[:, SHARED], sd_w.rearrange("(k p) d -> p k d", p=P)).then_inc(ld_ws, 16)

            def attention_io(q, r, last=False):
                t = num(q, r)
                sp.wait_ge(x2_s, t + 1)
                sp.dma_start(out_t[t], x2[:, r, :]).then_inc(st_x2[r], 16)
                if not last:
                    sp.dma_start(xin[:, r, :], x_t[t + SLOTS]).then_inc(ld_x[r], 16)
                sp.wait_ge(xn_s, t + 1)
                sp.dma_start(xn_t[t], xn[:, r, :]).then_inc(st_xn[r], 16)

            with sp.Fori(0, B - 1) as b:
                for r in range(RT):
                    attention_io(b, r)
            for r in range(RT):
                attention_io(B - 1, r, last=True)

            def shared_load(q, r):
                n = num(q, r)
                if isinstance(q, int) and q == 0:
                    sp.wait_ge(st_x2[r], 16 * B)
                else:
                    sp.wait_ge(y_s, n - SLOTS + 1)
                    sp.wait_ge(jxT_ps, n - SLOTS + 1)
                sp.wait_ge(st_xn[r], 16 * B)
                sp.dma_start(xg[:, r, :], xn_t[n]).then_inc(ld_xg[r], 16)
                sp.dma_start(x2[:, r, :], out_t[n]).then_inc(ld_x2[r], 16)

            def shared_store(q, r):
                n = num(q, r)
                sp.wait_ge(y_s, n + 1)
                sp.dma_start(out_t[n], y[:, r, :]).then_inc(st_y[r], 16)

            for r in range(SLOTS):
                shared_load(0, r)
            with sp.Fori(0, TILES // SLOTS - 1) as q:
                for r in range(SLOTS):
                    shared_store(q, r)
                    shared_load(q + 1, r)
            for r in range(SLOTS):
                shared_store(TILES // SLOTS - 1, r)

        @block.gpsimd
        def _(pool):
            steps = [0]

            def then(ins):
                steps[0] += 1
                ins.then_inc(pool_step, 1)
                pool.wait_ge(pool_step, steps[0])

            g = nc.gpsimd
            then(g.memset(ident[:], 0.0))
            then(g.affine_select(out=ident[:], in_=ident[:], compare_op=ALU.not_equal, fill=1.0, base=0,
                                 pattern=[[-1, P]], channel_multiplier=1))
            g.memset(ones[:], 1.0)
            g.memset(mhalf[:], -0.5).then_inc(c_pool, 1)
            zeros = xT[:].rearrange("p s k t -> p (s k t)")[:, 0:D]
            then(g.memset(zeros, 0.0))
            g.dma_start(out_t[TILES], zeros).then_inc(st_trash, 16)
            for e in range(E):
                act_w = gate_up_w[e].rearrange("(k p) f -> p k f", p=P)
                g.dma_start(gu[:, e], act_w).then_inc(ld_w, 16)
                g.dma_start(dn[:, e], down_w[e].rearrange("(k p) d -> p k d", p=P)).then_inc(ld_w, 16)
            pool.wait_ge(ld_mask, 32)
            g.tensor_scalar(mask_pen, mask_in[:], MASKED, None, ALU.mult).then_inc(pen_ready0, 1)
            g.tensor_scalar(kpad_pen, kpad_in[:], MASKED, None, ALU.mult).then_inc(pen_ready0, 1)
            pool.wait_ge(pen_ready0, 2)

            def penalty(q, r):
                if not (isinstance(q, int) and q == 0):
                    pool.wait_ge(max_s, before(pool, num(q, r) - SLOTS + 1))
                g.tensor_tensor(pen[:, r, :], mask_pen[:, r, :], kpad_pen[:, q, :], ALU.add).then_inc(pen_s, 1)

            def inv_std(q, r, stat_s, mv, ve, ve_s, rstd, rstd_s):
                t = num(q, r)
                pool.wait_ge(stat_s, before(pool, t + 1))
                g.tensor_scalar(ve[:, r:r + 1], mv[:, r, 1:2], EPS, None, ALU.add).then_inc(ve_s, 1)
                pool.wait_ge(ve_s, before(pool, t + 1))
                g.tensor_tensor(rstd[:, r:r + 1], ve[:, r:r + 1], mhalf[:], ALU.pow).then_inc(rstd_s, 1)

            def step(q, r, first=False, last=False):
                if not last:
                    nq, nr = shift(q, r, 1)
                    inv_std(nq, nr, xstat, mv1, ve1, ve1_s, rstd1, rstd1_s)
                    penalty(nq, nr)
                if not first:
                    pq, pr = shift(q, r, -1)
                    inv_std(pq, pr, mv2_s, mv2, ve2, ve2_s, rstd2, rstd2_s)

            inv_std(0, 0, xstat, mv1, ve1, ve1_s, rstd1, rstd1_s)
            penalty(0, 0)
            step(0, 0, first=True)
            for r in range(1, RT):
                step(0, r)
            with pool.Fori(1, B - 1) as b:
                for r in range(RT):
                    step(b, r)
            for r in range(RT):
                step(B - 1, r, last=(r == RT - 1))
            inv_std(B - 1, RT - 1, mv2_s, mv2, ve2, ve2_s, rstd2, rstd2_s)

            def iota(dst, pattern, base_, mult):
                return g.iota(dst, pattern=pattern, base=base_, channel_multiplier=mult,
                              allow_small_or_imprecise_dtypes=True)
            pool.wait_ge(max_s, TILES)
            g.memset(jprob[:, 0:TILES], 1.0)
            g.memset(jexpert[:, 0:TILES], SHARED)
            iota(idx8, [[0, TILES], [-1, E]], E, 0).then_inc(first_table, 1)
            iota(k128, [[0, E], [P, TILES]], 0, 0)
            iota(a128[:], [[P, NG]], 1, 0)
            iota(tok1[:], [[0, K], [P, TILES]], 1, 1)
            iota(iota1[:], [[1, P]], 1, 0)
            iota(pidx[:], [[0, 1]], T + 1, 1)
            then(g.memset(triangle[:], 1.0))
            g.affine_select(out=triangle[:], in_=triangle[:], compare_op=ALU.is_gt, fill=0.0, base=0,
                            pattern=[[1, P]], channel_multiplier=-1).then_inc(consts_s, 1)

            pool.wait_ge(G_s, 1)
            pool.wait_ge(prob_s, 1)
            then(g.tensor_tensor(R[:, :, 0], G[:, :, 0:ROUTED], G[:, :, 1:NG], ALU.subtract))
            then(g.tensor_tensor(R[:, :, 1], R[:, :, 0],
                                 prob[:].rearrange("p k t -> p (k t)").unsqueeze(2).to_broadcast([P, K * TILES, ROUTED]),
                                 ALU.mult))
            g.tensor_tensor(R[:, :, 0], R[:, :, 0],
                            tok1[:].rearrange("p k t -> p (k t)").unsqueeze(2).to_broadcast([P, K * TILES, ROUTED]),
                            ALU.mult).then_inc(R_s, 1)
            pool.wait_ge(table_s, 1)

            def gather(q, r):
                n = num(q, r)
                pool.wait_ge(jxT_ps, before(pool, n - SLOTS + 1))
                g.tensor_copy(gidx[:, r, :], jgather[:, bass.ds(n - TILES, 1)]).then_inc(gidx_s, 1)
                pool.wait_ge(gidx_s, before(pool, n - TILES + 1))
                g.indirect_dma_start(
                    out=xg[:, r, :], out_offset=None, in_=xn_dram,
                    in_offset=bass.IndirectOffsetOnAxis(ap=gidx[:, r, :], axis=0),
                    bounds_check=T - 1).then_inc(gt_xg[r], 16)

            def scatter(q, r, after_scatter=True):
                n = num(q, r)
                g.tensor_copy(sidx[:, r, :], jscatter[:, bass.ds(n - TILES, 1)]).then_inc(sidx_s, 1)
                pool.wait_ge(sidx_s, before(pool, n - TILES + 1))
                pool.wait_ge(y_s, before(pool, n + 1))
                if after_scatter:
                    pq, pr = shift(q, r, -1)
                    pool.wait_ge(add_y[pr], before(pool, 16 * (pq - J0 + 1)))
                g.indirect_dma_start(
                    out=out, out_offset=bass.IndirectOffsetOnAxis(ap=sidx[:, r, :], axis=0),
                    in_=y[:, r, :], in_offset=None, bounds_check=T + P - 1, compute_op=ALU.add).then_inc(add_y[r], 16)

            for r in range(SLOTS):
                gather(J0, r)
            for r in range(SLOTS):
                pool.wait_ge(st_y[r], 16 * J0)
            pool.wait_ge(st_trash, 16)
            QL = ROUTED // SLOTS
            for r in range(SLOTS):
                scatter(J0, r, after_scatter=(r > 0))
                gather(J0 + 1, r)
            with pool.Fori(J0 + 1, J0 + QL - 1) as q:
                for r in range(SLOTS):
                    scatter(q, r)
                    gather(q + 1, r)
            for r in range(SLOTS):
                scatter(J0 + QL - 1, r)
                if r < ROUTED % SLOTS:
                    gather(J0 + QL, r)
            for r in range(ROUTED % SLOTS):
                scatter(J0 + QL, r)
            for r in range(SLOTS):
                pool.wait_ge(add_y[r], 16 * (QL + (1 if r < ROUTED % SLOTS else 0)))

        @block.scalar
        def _(act):
            a = nc.scalar
            act.dma_start(mask_in[:], mask.rearrange("(r p) s -> p r s", p=P)).then_inc(ld_mask, 16)
            act.dma_start(kpad_in[:].rearrange("p b s -> p (b s)"),
                          kpad.rearrange("b s -> (b s)").partition_broadcast(P)).then_inc(ld_mask, 16)
            act.wait_ge(ld_small, 64)
            a.mul(bqk[:, 0:1], bqk[:, 0:1], SCALING).then_inc(bq_ready, 1)
            act.wait_ge(wT_ps, 1)
            a.copy(wqkT[:].rearrange("p w o -> p (w o)"), ps_proj[0][:, 0:2 * H]).then_inc(wT_ready, 1)
            act.wait_ge(bq_ready, 1)
            for b in range(B):
                act.wait_ge(ctxT_ps, b + 1)
                a.copy(ctxT[:, b % 2, :], ps_ctxT[:]).then_inc(ctxT_ready, 1)
                for w, dst in enumerate((qT, kT)):
                    act.wait_ge(proj_ps, 2 * b + w + 1)
                    a.activation(dst[:, b * S:(b + 1) * S], ps_proj[w][:], ACT.Identity, bias=bqk[:, w:w + 1],
                                 scale=SCALING if w == 0 else 1.0).then_inc(proj_ready, 1)

            def q_copy(q, r):
                t = num(q, r)
                if not (isinstance(q, int) and q == 0):
                    act.wait_ge(score_ps, t - SLOTS + 1)
                a.copy(q_tile[:, r, :], qT[:, bass.ds(P * t, P)]).then_inc(q_ready, 1)

            def expo(q, r):
                t = num(q, r)
                act.wait_ge(nbias_s, t + 1)
                a.activation(sc[:, r, :], sc[:, r, :], ACT.Exp, bias=nbias[:, r:r + 1], scale=rstd1[:, r:r + 1],
                             accum_out=rowsum[:, r:r + 1]).then_inc(exp_s, 1)

            def xnT_copy(q, r):
                t = num(q, r)
                act.wait_ge(xnT_ps, t + 1)
                a.copy(xT[:, r % 2].rearrange("p k t -> p (k t)"), ps_xnT[r % 2][:]).then_inc(xnT_ready, 1)

            def step(q, r, drop_q=False):
                expo(q, r)
                tq, tr = shift(q, r, -2)
                if not early(tq):
                    xnT_copy(tq, tr)
                if not drop_q:
                    q_copy(*shift(q, r, 2))

            act.wait_ge(proj_ready, 2 * B)
            act.wait_ge(st_trash, 16)
            q_copy(0, 0)
            q_copy(0, 1)
            for t in range(HEAD):
                step(t // RT, t % RT)
            with act.Fori(1, LOOP_END) as b:
                for d in range(RT):
                    step(*shift(b, LAG, d))
            for t in range(TILES - LAG, TILES):
                step(t // RT, t % RT, drop_q=True)
            xnT_copy(B - 1, RT - 2)
            xnT_copy(B - 1, RT - 1)
            act.wait_ge(logit_ps, TILES)
            a.copy(lg[:].rearrange("p t e -> p (t e)"), ps_logit[:, 0:TILES * E]).then_inc(lg_s, 1)

            def jxT_copy(q, r):
                n = num(q, r)
                act.wait_ge(jxT_ps, n + 1)
                a.copy(xT[:, r % 2].rearrange("p k t -> p (k t)"), ps_xT[:]).then_inc(jxT_s, 1)

            def silu(q, r):
                n = num(q, r)
                act.wait_ge(g_ps, n + 1)
                a.activation(sg[:, r % 2, :], ps_g[r % 2][:, 0:I], ACT.Silu,
                             scale=jprob[:, bass.ds(n, 1)]).then_inc(silu_s, 1)

            def job_step(q, r, last=False):
                silu(q, r)
                if not last:
                    jxT_copy(*shift(q, r, 1))

            act.wait_ge(first_table, 1)
            jxT_copy(0, 0)
            act.wait_ge(top_s, 1)
            a.activation(pexp[:], top[:], ACT.Exp, scale=-1.0).then_inc(pexp_s, 1)
            job_step(0, 0)
            job_step(0, 1)
            act.wait_ge(rank_ps, 1)
            a.copy(rank.rearrange("p a t e -> p (a t e)"), ps_rank[:, 0:2 * TILES * E]).then_inc(rank_s, 1)
            job_step(0, 2)
            job_step(0, 3)
            for r in range(SLOTS):
                job_step(1, r)
            job_step(2, 0)
            job_step(2, 1)
            act.wait_ge(map_ps, 1)
            a.copy(amap[:].rearrange("p a j -> p (a j)"), ps_map[:, 0:2 * ROUTED]).then_inc(map_s, 1)
            job_step(2, 2)
            job_step(2, 3)
            for r in range(SLOTS):
                job_step(3, r)
            act.wait_ge(table_s, 1)
            QF = JOBS // SLOTS
            with act.Fori(TILES // SLOTS, QF) as q:
                for r in range(SLOTS):
                    job_step(q, r)
            for r in range(JOBS % SLOTS):
                job_step(QF, r, last=(r == JOBS % SLOTS - 1))

        @block.vector
        def _(dve):
            v = nc.vector

            def stats(q, r, src, arrived, arrived_at, bn, bn_s, mv, mv_s):
                t = num(q, r)
                dve.wait_ge(arrived, arrived_at)
                v.bn_stats(bn[:, r, :], src[:, r, :]).then_inc(bn_s, 1)
                dve.wait_ge(bn_s, before(dve, t + 1))
                v.bn_aggr(mv[:, r, :], bn[:, r, :]).then_inc(mv_s, 1)

            def x_stats(q, r):
                stats(q, r, xin, ld_x[r], 16 * (q + 1), bn1, bn1_s, mv1, xstat)

            def scores(q, r):
                t = num(q, r)
                dve.wait_ge(score_ps, t + 1)
                dve.wait_ge(xstat, t + 1)
                v.scalar_tensor_tensor(sc[:, r, :], xin[:, r, :], mv1[:, r, 0:1], ps_score[r % 2][:],
                                       ALU.subtract, ALU.mult).then_inc(raw_s, 1)
                dve.wait_ge(raw_s, before(dve, t + 1))
                dve.wait_ge(pen_s, before(dve, t + 1))
                v.tensor_tensor_reduce(out=sc[:, r, :], in0=sc[:, r, :], in1=pen[:, r, :], scale=1.0, scalar=-BIG,
                                       op0=ALU.add, op1=ALU.max, accum_out=rowmax[:, r:r + 1]).then_inc(max_s, 1)
                dve.wait_ge(max_s, t + 1)
                dve.wait_ge(rstd1_s, t + 1)
                v.scalar_tensor_tensor(nbias[:, r:r + 1], rowmax[:, r:r + 1], -1.0, rstd1[:, r:r + 1],
                                       ALU.mult, ALU.mult).then_inc(nbias_s, 1)

            def residual(q, r):
                t = num(q, r)
                dve.wait_ge(exp_s, t + 1)
                v.scalar_tensor_tensor(rowsum[:, r:r + 1], rowmax[:, r:r + 1], MASKED / 2, rowsum[:, r:r + 1],
                                       ALU.is_gt, ALU.mult).then_inc(rsum_s, 1)
                dve.wait_ge(rsum_s, t + 1)
                v.reciprocal(rsraw[:, r:r + 1], rowsum[:, r:r + 1]).then_inc(rsraw_s, 1)
                dve.wait_ge(rsraw_s, t + 1)
                v.scalar_tensor_tensor(rinv[:, r:r + 1], rowmax[:, r:r + 1], MASKED / 2, rsraw[:, r:r + 1],
                                       ALU.is_gt, ALU.mult).then_inc(rinv_s, 1)
                dve.wait_ge(rinv_s, t + 1)
                if not (isinstance(q, int) and q == 0):
                    dve.wait_ge(st_x2[r], 16 * q)
                v.scalar_tensor_tensor(x2[:, r, :], sc[:, r, :], rinv[:, r:r + 1], xin[:, r, :],
                                       ALU.mult, ALU.add).then_inc(x2_s, 1)
                stats(q, r, x2, x2_s, t + 1, bn2, bn2_s, mv2, mv2_s)

            def normal(q, r):
                t = num(q, r)
                dve.wait_ge(rstd2_s, t + 1)
                if not (isinstance(q, int) and q == 0):
                    dve.wait_ge(st_xn[r], 16 * q)
                    dve.wait_ge(xnT_ps, t - SLOTS + 1)
                v.tensor_scalar(xn[:, r, :], x2[:, r, :], mv2[:, r, 0:1], rstd2[:, r:r + 1],
                                ALU.subtract, ALU.mult).then_inc(xn_s, 1)

            def step(q, r, last=False):
                if not last:
                    x_stats(*shift(q, r, 1))
                scores(q, r)
                pq, pr = shift(q, r, -1)
                if not early(pq):
                    residual(pq, pr)
                pq, pr = shift(q, r, -2)
                if not early(pq):
                    normal(pq, pr)

            x_stats(0, 0)
            for t in range(HEAD):
                step(t // RT, t % RT)
            with dve.Fori(1, LOOP_END) as b:
                for d in range(RT):
                    step(*shift(b, LAG, d))
            for t in range(TILES - LAG, TILES):
                step(t // RT, t % RT, last=(t == TILES - 1))
            residual(B - 1, RT - 1)
            normal(B - 1, RT - 2)
            normal(B - 1, RT - 1)

            steps = [0]

            def then(ins):
                steps[0] += 1
                ins.then_inc(dve_step, 1)
                dve.wait_ge(dve_step, steps[0])

            def wide(column, shape):
                return column.unsqueeze(2).to_broadcast(shape)

            def choose():
                dve.wait_ge(first_table, 1)
                dve.wait_ge(lg_s, 1)
                src = lg[:]
                for k in range(K):
                    then(v.tensor_reduce(top[:, k], src, X, ALU.max))
                    then(v.tensor_tensor(eq, src, wide(top[:, k], [P, TILES, E]), ALU.is_equal))
                    then(v.tensor_tensor(eq, eq, idx8, ALU.mult))
                    then(v.tensor_reduce(best[:], eq, X, ALU.max))
                    then(v.tensor_tensor(oh[:, k], idx8, wide(best[:], [P, TILES, E]), ALU.is_equal))
                    if k == 0:
                        then(v.scalar_tensor_tensor(lg2, oh[:, 0], -BIG, lg[:], ALU.mult, ALU.add))
                        src = lg2
                v.tensor_scalar(top[:], top[:], -88.0, BIG, ALU.max, ALU.min).then_inc(top_s, 1)
                v.tensor_tensor(ohs[:], oh[:, 0], oh[:, 1], ALU.add).then_inc(oh_s, 1)

            def count():
                dve.wait_ge(consts_s, 1)
                dve.wait_ge(rank_s, 1)
                dve.wait_ge(pexp_s, 1)
                then(v.tensor_scalar(prob[:], pexp[:], 1.0, None, ALU.add))
                v.reciprocal(prob[:], prob[:]).then_inc(prob_s, 1)
                v.tensor_reduce(cnt[:], rank[:, 1].rearrange("p t e -> p e t"), X, ALU.add)
                then(v.tensor_copy(cum[:, 0], rank[:, 1]))
                then(v.tensor_tensor(cmp, wide(cnt[:], [P, E, TILES]), k128, ALU.is_gt))
                then(v.tensor_reduce(ntile[:, 0], cmp, X, ALU.add))
                for i, d in enumerate((1, 2, 4)):
                    v.tensor_copy(ntile[:, i + 1, 0:d], ntile[:, i, 0:d])
                    then(v.tensor_tensor(ntile[:, i + 1, d:], ntile[:, i, d:], ntile[:, i, 0:E - d], ALU.add))
                then(v.tensor_tensor(base[:], ntile[:, 3], ntile[:, 0], ALU.subtract))

            def places():
                side = 0
                for d in (1, 2, 4, 8):
                    v.tensor_copy(cum[:, 1 - side, 0:d], cum[:, side, 0:d])
                    then(v.tensor_tensor(cum[:, 1 - side, d:], cum[:, side, d:], cum[:, side, 0:TILES - d], ALU.add))
                    side = 1 - side
                then(v.tensor_tensor(place, cum[:, side], rank[:, 1], ALU.subtract))
                then(v.tensor_scalar(base[:], base[:], float(P), 1.0, ALU.mult, ALU.add))
                then(v.tensor_tensor(place, place, rank[:, 0], ALU.add))
                then(v.tensor_tensor(place, place, base[:].unsqueeze(1).to_broadcast([P, TILES, E]), ALU.add))
                for k in range(K):
                    then(v.tensor_tensor(eq, oh[:, k], place, ALU.mult))
                    then(v.tensor_reduce(slot1[:, k], eq, X, ALU.add))

            slots = slot1[:].rearrange("p k t -> p (k t)")

            def job_of_choice():
                then(v.tensor_tensor(G, wide(slots, [P, K * TILES, NG]),
                                     a128[:].unsqueeze(1).to_broadcast([P, K * TILES, NG]), ALU.is_ge))
                v.tensor_reduce(acol[:], G[:, :, 1:NG], X, ALU.add).then_inc(G_s, 1)
                dve.wait_ge(G_s, 1)
                then(v.scalar_tensor_tensor(bcol[:], acol[:], -float(P), slots, ALU.mult, ALU.add))

            def row_of_choice(half):
                c0, c1 = half * TILES, (half + 1) * TILES
                v.tensor_tensor(OB[:, c0:c1], iota1[:].unsqueeze(1).to_broadcast([P, TILES, P]),
                                wide(bcol[:, c0:c1], [P, TILES, P]), ALU.is_equal).then_inc(OB_s, 1)

            def job_experts():
                then(v.tensor_scalar(ntile[:, 0], ntile[:, 3], float(P), 1.0, ALU.mult, ALU.add))
                then(v.tensor_tensor(ecmp[:], wide(a128[:, 0:ROUTED], [P, ROUTED, E]),
                                     ntile[:, 0].unsqueeze(1).to_broadcast([P, ROUTED, E]), ALU.is_ge))
                then(v.tensor_reduce(efl[:], ecmp[:], X, ALU.add))
                v.tensor_scalar(jexpert[:, TILES:JOBS], efl[:], float(E - 1), None, ALU.min)

            def tables():
                dve.wait_ge(map_s, 1)
                then(v.tensor_scalar(hole[:], amap[:, 0], 0.0, None, ALU.is_equal))
                v.tensor_scalar(jgather[:], amap[:, 0], -1.0, 0.0, ALU.add, ALU.max)
                then(v.scalar_tensor_tensor(jf[:], hole[:], pidx[:], amap[:, 0], ALU.mult, ALU.add))
                v.tensor_copy(jprob[:, TILES:JOBS], amap[:, 1])
                v.tensor_scalar(jscatter[:], jf[:], -1.0, None, ALU.add).then_inc(table_s, 1)

            def hT_copy(q, r):
                n = num(q, r)
                dve.wait_ge(hT_ps, n + 1)
                if n is not None and not (isinstance(q, int) and num(q, r) < 2):
                    dve.wait_ge(y_ps, n - 1)
                v.tensor_copy(hT[:, r % 2].rearrange("p c t -> p (c t)"), ps_hT[:, 0:I]).then_inc(hT_s, 1)

            def gated(q, r):
                n = num(q, r)
                dve.wait_ge(silu_s, n + 1)
                if not (isinstance(q, int) and num(q, r) < 2):
                    dve.wait_ge(hT_ps, n - 1)
                v.scalar_tensor_tensor(h[:, r % 2, :], ps_g[r % 2][:, I:2 * I], jprob[:, bass.ds(n, 1)],
                                       sg[:, r % 2, :], ALU.mult, ALU.mult).then_inc(h_s, 1)

            def y_out(q, r, shared):
                n = num(q, r)
                dve.wait_ge(y_ps, n + 1)
                if isinstance(q, int) and 0 < q <= J0:
                    dve.wait_ge(st_y[r], 16 * q)
                elif not isinstance(q, int) or q > J0:
                    dve.wait_ge(add_y[r], 16 * (q - J0))
                if shared:
                    dve.wait_ge(ld_x2[r], 16 * (q + 1))
                    v.tensor_tensor(y[:, r, :], ps_y[r % 2][:], x2[:, r, :], ALU.add).then_inc(y_s, 1)
                else:
                    v.tensor_copy(y[:, r, :], ps_y[r % 2][:]).then_inc(y_s, 1)

            def job_step(q, r, shared=False):
                pq, pr = shift(q, r, -1)
                if not early(pq):
                    hT_copy(pq, pr)
                gated(q, r)
                if not early(pq):
                    y_out(pq, pr, shared)

            choose()
            for r in range(3):
                job_step(0, r, shared=True)
            count()
            job_step(0, 3, shared=True)
            places()
            job_step(1, 0, shared=True)
            job_of_choice()
            job_step(1, 1, shared=True)
            row_of_choice(0)
            job_step(1, 2, shared=True)
            row_of_choice(1)
            job_step(1, 3, shared=True)
            job_experts()
            job_step(2, 0, shared=True)
            job_step(2, 1, shared=True)
            job_step(2, 2, shared=True)
            tables()
            job_step(2, 3, shared=True)
            for r in range(SLOTS):
                job_step(3, r, shared=True)
            QF = JOBS // SLOTS
            dve.wait_ge(table_s, 1)
            job_step(TILES // SLOTS, 0, shared=True)
            for r in range(1, SLOTS):
                job_step(TILES // SLOTS, r)
            with dve.Fori(TILES // SLOTS + 1, QF) as q:
                for r in range(SLOTS):
                    job_step(q, r)
            for r in range(JOBS % SLOTS):
                job_step(QF, r)
            lq, lr = QF, JOBS % SLOTS - 1
            hT_copy(lq, lr)
            y_out(lq, lr, False)

        @block.tensor
        def _(pe):
            tn = nc.tensor
            pe.wait_ge(c_pool, 1)
            pe.wait_ge(ld_small, 64)
            for w in range(2):
                last = tn.transpose(ps_proj[0][:, w * H:(w + 1) * H], wqk[:, w, :], ident[:])
            last.then_inc(wT_ps, 1)
            pe.wait_ge(ld_ctx, 16)
            for b in range(B):
                if b:
                    pe.wait_ge(ctxT_ready, b)
                for r in range(RT):
                    last = tn.transpose(ps_ctxT[:, r * P:(r + 1) * P], ctx_in[:, b * RT + r, :], ident[:])
                last.then_inc(ctxT_ps, 1)
                if b == 0:
                    pe.wait_ge(wT_ready, 1)
                pe.wait_ge(ctxT_ready, b + 1)
                for w in range(2):
                    if b:
                        pe.wait_ge(proj_ready, 2 * b - 1 + w)
                    tn.matmul(ps_proj[w][:], wqkT[:, w, :], ctxT[:, b % 2, :], start=True, stop=True).then_inc(proj_ps, 1)
            pe.wait_ge(proj_ready, 2 * B)
            pe.wait_ge(ld_rw, 16)

            def scores(q, r):
                t = num(q, r)
                pe.wait_ge(q_ready, t + 1)
                if not (isinstance(q, int) and num(q, r) < 2):
                    pe.wait_ge(raw_s, t - 1)
                tn.matmul(ps_score[r % 2][:], q_tile[:, r, :], kT[:, bass.ds(S * q, S)], start=True,
                          stop=True).then_inc(score_ps, 1)

            def xn_transpose(q, r):
                t = num(q, r)
                pe.wait_ge(xn_s, t + 1)
                if not (isinstance(q, int) and num(q, r) < 2):
                    pe.wait_ge(xnT_ready, t - 1)
                for k in range(KC):
                    last = tn.transpose(ps_xnT[r % 2][:, k * P:(k + 1) * P], xn[:, r, k * P:(k + 1) * P], ident[:])
                last.then_inc(xnT_ps, 1)

            def logits(q, r):
                t = num(q, r)
                pe.wait_ge(xnT_ready, t + 1)
                for k in range(KC):
                    last = tn.matmul(ps_logit[:, bass.ds(E * t, E)], xT[:, r % 2, k, :], rw[:, k, :],
                                     start=(k == 0), stop=(k == KC - 1))
                last.then_inc(logit_ps, 1)

            def step(q, r, last=False):
                if not last:
                    scores(*shift(q, r, 1))
                pq, pr = shift(q, r, -2)
                if not early(pq):
                    xn_transpose(pq, pr)
                    logits(pq, pr)

            scores(0, 0)
            for t in range(HEAD):
                step(t // RT, t % RT)
            with pe.Fori(1, LOOP_END) as b:
                for d in range(RT):
                    step(*shift(b, LAG, d))
            for t in range(TILES - LAG, TILES):
                step(t // RT, t % RT, last=(t == TILES - 1))
            for r in (RT - 2, RT - 1):
                xn_transpose(B - 1, r)
                logits(B - 1, r)

            def x_transpose(q, r):
                n = num(q, r)
                if isinstance(q, int) and q < J0:
                    pe.wait_ge(ld_xg[r], 16 * (q + 1))
                else:
                    pe.wait_ge(gt_xg[r], 16 * (q - J0 + 1))
                if not (isinstance(q, int) and num(q, r) == 0):
                    pe.wait_ge(jxT_s, n)
                for k in range(KC):
                    last = tn.transpose(ps_xT[:, k * P:(k + 1) * P], xg[:, r, k * P:(k + 1) * P], ident[:])
                last.then_inc(jxT_ps, 1)

            def expert(n):
                return pe.value_load(jexpert[0:1, bass.ds(n, 1)], min_val=0, max_val=E)

            def gate_up(q, r):
                n = num(q, r)
                e = expert(n)
                pe.wait_ge(jxT_s, n + 1)
                if not (isinstance(q, int) and num(q, r) < 2):
                    pe.wait_ge(h_s, n - 1)
                for k in range(KC):
                    last = tn.matmul(ps_g[r % 2][:], xT[:, r % 2, k, :], gu[:, e, k, :], start=(k == 0), stop=(k == KC - 1))
                last.then_inc(g_ps, 1)

            def h_transpose(q, r):
                n = num(q, r)
                pe.wait_ge(h_s, n + 1)
                if not (isinstance(q, int) and num(q, r) == 0):
                    pe.wait_ge(hT_s, n)
                for c in range(IC):
                    last = tn.transpose(ps_hT[:, c * P:(c + 1) * P], h[:, r % 2, c * P:(c + 1) * P], ident[:])
                last.then_inc(hT_ps, 1)

            def down(q, r):
                n = num(q, r)
                e = expert(n)
                pe.wait_ge(hT_s, n + 1)
                if not (isinstance(q, int) and num(q, r) < 2):
                    pe.wait_ge(y_s, n - 1)
                for c in range(IC):
                    last = tn.matmul(ps_y[r % 2][:], hT[:, r % 2, c, :], dn[:, e, c, :], start=(c == 0), stop=(c == IC - 1))
                last.then_inc(y_ps, 1)

            def job_step(q, r, last=False):
                pq, pr = shift(q, r, -1)
                if not early(pq):
                    h_transpose(pq, pr)
                gate_up(q, r)
                if not last:
                    x_transpose(*shift(q, r, 1))
                if not early(pq):
                    down(pq, pr)

            pe.wait_ge(first_table, 1)
            pe.wait_ge(raw_s, TILES)
            x_transpose(0, 0)
            pe.wait_ge(ld_ws, 16 * 3)
            job_step(0, 0)
            job_step(0, 1)
            pe.wait_ge(consts_s, 1)
            pe.wait_ge(oh_s, 1)
            tn.matmul(ps_rank[:, 0:TILES * E], triangle[:], ohs[:].rearrange("p t e -> p (t e)"), start=True, stop=True)
            tn.matmul(ps_rank[:, TILES * E:2 * TILES * E], ones[:], ohs[:].rearrange("p t e -> p (t e)"),
                      start=True, stop=True).then_inc(rank_ps, 1)
            for n in range(2, 10):
                job_step(n // SLOTS, n % SLOTS)
            pe.wait_ge(R_s, 1)
            pe.wait_ge(OB_s, 2)
            for i in range(K * TILES):
                last = tn.matmul(ps_map[:, 0:2 * ROUTED], OB[:, i, :], R[:, i].rearrange("p a j -> p (a j)"),
                                 start=(i == 0), stop=(i == K * TILES - 1))
            last.then_inc(map_ps, 1)
            for n in range(10, TILES):
                if n == TILES - 1:
                    pe.wait_ge(table_s, 1)
                    pe.wait_ge(ld_w, 16 * 2 * E)
                job_step(n // SLOTS, n % SLOTS)
            QF = JOBS // SLOTS
            with pe.Fori(TILES // SLOTS, QF) as q:
                for r in range(SLOTS):
                    job_step(q, r)
            for r in range(JOBS % SLOTS):
                job_step(QF, r, last=(r == JOBS % SLOTS - 1))
            h_transpose(QF, JOBS % SLOTS - 1)
            down(QF, JOBS % SLOTS - 1)


_INS = ['x', 'ctx_512', 'mask_SxS2_bk1', 'mask_BxS2_bf0', 'L0_xattn_Wq', 'L0_xattn_bq', 'L0_xattn_Wk',
        'L0_xattn_bk', 'L0_ffn_router_w', 'L0_ffn_gate_up_w', 'L0_ffn_down_w', 'L0_ffn_shared_gate_w',
        'L0_ffn_shared_up_w', 'L0_ffn_shared_down_w']


def kernel(**inputs):
    import concourse.bacc as _bacc
    from concourse.bass_utils import run_bass_kernel_spmd as _run

    nc = _bacc.Bacc("TRN2", target_bir_lowering=False, num_devices=1)
    arrays, args = {}, []
    for name in _INS:
        a = np.ascontiguousarray(inputs[name])
        arrays[f"in_{name}"] = a
        args.append(nc.dram_tensor(f"in_{name}", a.shape, mybir.dt.from_np(a.dtype), kind="ExternalInput").ap())
    args.append(nc.dram_tensor("out_rows", (T + P, D), mybir.dt.float32, kind="ExternalOutput").ap())
    build(nc, *args)
    r = _run(nc, [arrays], core_ids=[0])
    return r.results[0]["out_rows"][:T].reshape(B, S, D)
```

```python
import numpy as np
import concourse.bass as bass
from concourse import mybir
from contextlib import ExitStack

P = 128
B, S, D, H = 4, 512, 512, 128
T = B * S
TILES = T // P
RT = S // P
KC = D // P
E, K, I = 8, 2, 256
IC = I // P
SHARED = 0
LATE = E // 2 + 2
CH = 2
ROUTED = (K * T + E * (P - 1)) // P
JOBS = TILES + ROUTED
EPS = 1e-5
SCALING = float(H) ** -0.5
BIG = 3e38
MASKED = -1e30
LAG = 2
HEAD = RT + LAG
LOOP_END = B - 1
SCRATCH = 2048
SLOTS = 4


def build(nc, x, ctx, mask, kpad, wq, bq, wk, bk, router_w, gate_up_w, down_w, sg_w, su_w, sd_w, out):
    f32r = mybir.dt.float32r
    f32, bf16, i32, u8 = mybir.dt.float32, mybir.dt.bfloat16, mybir.dt.int32, mybir.dt.uint8
    ALU, ACT, X = mybir.AluOpType, mybir.ActivationFunctionType, mybir.AxisListType.X

    x_t = x.rearrange("b (r p) d -> (b r) p d", p=P)
    out_t = out.rearrange("(t p) d -> t p d", p=P)
    xn_dram = nc.dram_tensor("xn_rows", (T, D), f32, kind="Internal").ap()
    xn_t = xn_dram.rearrange("(t p) d -> t p d", p=P)

    stack = ExitStack()
    with stack:
        def sb(name, shape, dt=f32):
            return stack.enter_context(nc.sbuf_tensor(name, shape, dt))

        def sem(name):
            return stack.enter_context(nc.semaphore(name))

        def sems(name, n=SLOTS):
            return [sem(f"{name}{i}") for i in range(n)]

        LN = E + 1 - LATE
        under = ExitStack()

        def u(name, shape, dt=f32):
            return under.enter_context(nc.sbuf_tensor(name, shape, dt))

        u("gu_hi_head", [P, LATE, KC, 2 * I])
        qkT = u("qkT", [P, 2 * T])
        ctx_in = u("ctx_in", [P, TILES, H])
        u("dn_hi_head", [P, LATE, IC, D])
        ctxT = u("ctxT", [P, 2, S])
        mask_in = u("mask_in", [P, RT, S], u8)
        kpad_in = u("kpad_in", [P, B, S], u8)
        q_tile = u("q_tile", [P, SLOTS, P])
        u("dn_hi_rest", [P, LN * IC * D - 2 * S - (RT + B) * S // 4 - SLOTS * P])
        u("gu_lo_head", [P, LATE, KC, 2 * I], bf16)
        pens = u("pens", [P, RT + B + SLOTS, S], bf16)
        u("dn_lo_head", [P, LATE, IC, D], bf16)
        wqk = u("wqk", [P, 2, H])
        wqkT = u("wqkT", [P, 2, H])
        oh = u("oh", [P, K, TILES, E])
        ohs = u("ohs", [P, TILES, E])
        triangle = u("triangle", [P, P])
        iota1 = u("iota1", [P, P])
        u("dn_lo_rest", [P, LN * IC * D - 8 * H - 2 * K * TILES * E - 2 * TILES * E - 4 * P], bf16)
        xT = u("xT", [P, 2, KC, P])
        xn = u("xn", [P, SLOTS, D])
        under.close()
        gu_hi = sb("gu_hi", [P, E + 1, KC, 2 * I], f32r)
        dn_hi = sb("dn_hi", [P, E + 1, IC, D], f32r)
        gu_lo = sb("gu_lo", [P, E + 1, KC, 2 * I], bf16)
        dn_lo = sb("dn_lo", [P, E + 1, IC, D], bf16)
        x_hi = sb("x_hi", [P, 2, KC, P], f32r)
        x_lo = sb("x_lo", [P, 2, KC, P], f32r)
        h_lo = sb("h_lo", [P, 2, IC, P], f32r)
        x_bf = sb("x_bf", [P, 2, KC, P], bf16)
        mask_pen = pens[:, 0:RT]
        kpad_pen = pens[:, RT:RT + B]
        pen = pens[:, RT + B:]
        qT = qkT[:, 0:T]
        kT = qkT[:, T:2 * T]
        stage = sb("stage", [P, 3, CH, D])
        rw = sb("rw", [P, KC, E])
        bqk = sb("bqk", [P, 2])
        ident = sb("ident", [P, P])
        ones = sb("ones", [P, P])
        xin = sb("xin", [P, SLOTS, D])
        sc = sb("sc", [P, SLOTS, S])
        x2 = sb("x2", [P, SLOTS, D])
        bn1 = sb("bn1", [P, SLOTS, 6])
        mv1 = sb("mv1", [P, SLOTS, 2])
        bn2 = sb("bn2", [P, SLOTS, 6])
        mv2 = sb("mv2", [P, SLOTS, 2])
        ve1 = sb("ve1", [P, SLOTS])
        ve2 = sb("ve2", [P, SLOTS])
        rstd1 = sb("rstd1", [P, SLOTS])
        rstd2 = sb("rstd2", [P, SLOTS])
        rowmax = sb("rowmax", [P, SLOTS])
        nbias = sb("nbias", [P, SLOTS])
        rowsum = sb("rowsum", [P, SLOTS])
        rinv = sb("rinv", [P, SLOTS])
        mhalf = sb("mhalf", [P, 1])
        xg = sc
        y = xin
        h = sb("h", [P, 2, I])
        h_hi = sb("h_hi", [P, 2, IC, P], f32r)
        h_bf = sb("h_bf", [P, 2, IC, P], bf16)
        jprob = sb("jprob", [P, JOBS])
        jexpert = sb("jexpert", [P, JOBS], i32)
        jgather = sb("jgather", [P, ROUTED], i32)
        jscatter = sb("jscatter", [P, ROUTED], i32)
        gidx = sb("gidx", [P, SLOTS, 1], i32)
        sidx = sb("sidx", [P, SLOTS, 1], i32)
        NG = ROUTED + 1
        spare = [0]

        def old(name_, shape):
            n = int(np.prod(shape[1:]))
            at, spare[0] = spare[0], spare[0] + n
            letters = "abc"[:len(shape) - 1]
            return pens[:].rearrange("p r s -> p (r s)").bitcast(f32)[:, at:at + n].rearrange(
                f"p ({' '.join(letters)}) -> p {' '.join(letters)}", **dict(zip(letters[1:], shape[2:])))

        G = old("G", [P, K * TILES, NG])
        eq = old("eq", [P, TILES, E])
        key = old("key", [P, TILES, E])
        lg2 = old("lg2", [P, TILES, E])
        idx8 = old("idx8", [P, TILES, E])
        rank = old("rank", [P, 2, TILES, E])
        cum = old("cum", [P, 2, TILES, E])
        k128 = old("k128", [P, E, TILES])
        cmp = old("cmp", [P, E, TILES])
        place = old("place", [P, TILES, E])
        ecmp = old("ecmp", [P, ROUTED, E])
        lg = sb("lg", [P, TILES, E])
        top = sb("top", [P, K, TILES])
        best = sb("best", [P, TILES])
        prob = sb("prob", [P, K, TILES])
        pexp = sb("pexp", [P, K, TILES])
        cnt = sb("cnt", [P, E])
        ntile = sb("ntile", [P, 4, E])
        slot1 = sb("slot1", [P, K, TILES])
        base = sb("base", [P, E])
        a128 = sb("a128", [P, NG])
        acol = sb("acol", [P, K * TILES])
        bcol = sb("bcol", [P, K * TILES])
        tok1 = sb("tok1", [P, K, TILES])
        OB = qkT[:].rearrange("p (c j) -> p c j", j=P)
        R = stage[:].rearrange("p s c d -> p (s c d)")[:, 0:K * TILES * 2 * ROUTED].rearrange(
            "p (c m a) -> p c m a", m=2, a=ROUTED)
        efl = sb("efl", [P, ROUTED])
        amap = sb("amap", [P, 2, ROUTED])
        pidx = sb("pidx", [P, 1])
        hole = sb("hole", [P, ROUTED])
        jf = sb("jf", [P, ROUTED])

        bank = [stack.enter_context(nc.psum_tensor(f"bank{i}", [P, 512], f32)) for i in range(8)]
        ps_score = bank[0:2]
        ps_xnT = bank[2:4]
        ps_logit = bank[4]
        ps_ctxT = bank[7]
        ps_proj = bank[5:7]
        ps_g = bank[0:2]
        ps_xT = [bank[2], bank[7]]
        ps_hT = bank[3]
        ps_y = bank[5:7]
        ps_rank = bank[4]
        ps_map = bank[4]

        ld_ctx0 = sem("ld_ctx0")
        ld_ctx, ld_small, ld_mask, ld_rw = sem("ld_ctx"), sem("ld_small"), sem("ld_mask"), sem("ld_rw")
        ld_x, st_x2, st_xn = sems("ld_x"), sems("st_x2"), sems("st_xn")
        ld_xg, ld_x2, st_y = sems("ld_xg"), sems("ld_x2"), sems("st_y")
        gt_xg, add_y = sems("gt_xg"), sems("add_y")
        st_trash = sem("st_trash")
        ld_st = sems("ld_st", 3)
        hi_s, lo_s = sem("hi_s"), sem("lo_s")
        c_pool = sem("c_pool")
        c_zero = sem("c_zero")
        pen_ready0 = sem("pen_ready0")
        wT_ps, wT_ready, ctxT_ps, ctxT_ready, proj_ps, proj_ready = (
            sem("wT_ps"), sem("wT_ready"), sem("ctxT_ps"), sem("ctxT_ready"), sem("proj_ps"), sem("proj_ready"))
        bq_ready = sem("bq_ready")
        q_ready, score_ps, xstat, bn1_s, bn2_s, ve1_s, ve2_s = (
            sem("q_ready"), sem("score_ps"), sem("xstat"), sem("bn1_s"), sem("bn2_s"), sem("ve1_s"), sem("ve2_s"))
        rstd1_s, rstd2_s, pen_s, raw_s, max_s, nbias_s, exp_s, rinv_s, x2_s, mv2_s, xn_s = (
            sem("rstd1_s"), sem("rstd2_s"), sem("pen_s"), sem("raw_s"), sem("max_s"), sem("nbias_s"), sem("exp_s"),
            sem("rinv_s"), sem("x2_s"), sem("mv2_s"), sem("xn_s"))
        xnT_ps, xnT_ready, logit_ps = sem("xnT_ps"), sem("xnT_ready"), sem("logit_ps")
        jxT_ps, xhi_s, xbf_s, xlo_s, g_ps, silu_s, h_s, hT_ps, hhi_s, hbf_s, hlo_s, y_ps, y_s = (
            sem("jxT_ps"), sem("xhi_s"), sem("xbf_s"), sem("xlo_s"), sem("g_ps"), sem("silu_s"), sem("h_s"),
            sem("hT_ps"), sem("hhi_s"), sem("hbf_s"), sem("hlo_s"), sem("y_ps"), sem("y_s"))
        lg_s, top_s, pexp_s, oh_s, rank_ps, rank_s, map_ps, map_s, table_s = (
            sem("lg_s"), sem("top_s"), sem("pexp_s"), sem("oh_s"), sem("rank_ps"), sem("rank_s"),
            sem("map_ps"), sem("map_s"), sem("table_s"))
        consts_s, prob_s, G_s, R_s, OB_s = sem("consts_s"), sem("prob_s"), sem("G_s"), sem("R_s"), sem("OB_s")
        rsum_s, rsraw_s = sem("rsum_s"), sem("rsraw_s")
        gidx_s, sidx_s = sem("gidx_s"), sem("sidx_s")
        pool_step, dve_step = sem("pool_step"), sem("dve_step")
        first_table = sem("first_table")

        block = stack.enter_context(nc.Block())

        def shift(q, r, by):
            return q + (r + by) // SLOTS, (r + by) % SLOTS

        def before(engine, value):
            if not isinstance(value, int):
                value = engine.snap(engine.to_reg(value))
                engine.wait_ge(c_pool, 1)
            return value

        def num(q, r):
            return SLOTS * q + r

        J0 = TILES // SLOTS

        def early(q):
            return isinstance(q, int) and q < 0

        def third(pair, place, i):
            return pair[0][:, place, CH * i:CH * (i + 1), :] if i < 2 else pair[1][:, place]

        gu_src = gate_up_w.rearrange("e (k p) f -> e p k f", p=P)
        dn_src = down_w.rearrange("e (k p) d -> e p k d", p=P)

        def chunk_number(expert, i):
            return 3 * (expert + 1) + i

        def stage_weights(engine, expert, i):
            c = chunk_number(expert, i)
            engine.wait_ge(hi_s, c - 2)
            engine.wait_ge(lo_s, c - 2)
            src = gu_src[expert, :, CH * i:CH * (i + 1), :] if i < 2 else dn_src[expert]
            for a in range(CH):
                engine.dma_start(stage[:, i, a, :], src[:, a, :]).then_inc(ld_st[i], 16)

        @block.sync
        def _(sp):
            ctx_rows = ctx.rearrange("b (r p) h -> p (b r) h", p=P)
            sp.dma_start(wqk[:, 0, :], wq).then_inc(ld_small, 16)
            sp.dma_start(wqk[:, 1, :], wk).then_inc(ld_small, 16)
            sp.dma_start(ctx_in[:, 0:RT], ctx_rows[:, 0:RT]).then_inc(ld_ctx0, 16)
            sp.dma_start(bqk[:, 0:1], bq.rearrange("(p o) -> p o", o=1)).then_inc(ld_small, 16)
            sp.dma_start(bqk[:, 1:2], bk.rearrange("(p o) -> p o", o=1)).then_inc(ld_small, 16)
            sp.dma_start(xin[:, 0, :], x_t[0]).then_inc(ld_x[0], 16)
            sp.dma_start(ctx_in[:, RT:], ctx_rows[:, RT:]).then_inc(ld_ctx, 16)
            sp.dma_start(xin[:, 1, :], x_t[1]).then_inc(ld_x[1], 16)
            sp.dma_start(rw[:], router_w.rearrange("(k p) e -> p k e", p=P)).then_inc(ld_rw, 16)
            for i in range(2):
                for half, w in enumerate((sg_w, su_w)):
                    sp.dma_start(stage[:, i, :, half * I:(half + 1) * I],
                                 w.rearrange("(k p) f -> p k f", p=P)[:, CH * i:CH * (i + 1), :]).then_inc(ld_st[i], 16)
            sp.dma_start(stage[:, 2, 0, :], sd_w.rearrange("(k p) d -> p k d", p=P)[:, 0, :]).then_inc(ld_st[2], 16)
            sp.dma_start(stage[:, 2, 1, :], sd_w.rearrange("(k p) d -> p k d", p=P)[:, 1, :]).then_inc(ld_st[2], 16)
            for r in range(2, SLOTS):
                sp.dma_start(xin[:, r, :], x_t[r]).then_inc(ld_x[r], 16)

            def weights(expert, i):
                stage_weights(sp, expert, i)

            def attention_io(q, r, last=False):
                t = num(q, r)
                sp.wait_ge(x2_s, t + 1)
                sp.dma_start(out_t[t], x2[:, r, :]).then_inc(st_x2[r], 16)
                if not last:
                    sp.dma_start(xin[:, r, :], x_t[t + SLOTS]).then_inc(ld_x[r], 16)
                sp.wait_ge(xn_s, t + 1)
                sp.dma_start(xn_t[t], xn[:, r, :]).then_inc(st_xn[r], 16)

            with sp.Fori(0, B - 1) as b:
                for r in range(RT):
                    attention_io(b, r)
                    if r < 3:
                        weights(b, r)
            for r in range(RT):
                attention_io(B - 1, r, last=True)
                if r < 3:
                    weights(B - 1, r)

            def shared_load(q, r):
                n = num(q, r)
                if isinstance(q, int) and q == 0:
                    sp.wait_ge(st_x2[r], 16 * B)
                else:
                    sp.wait_ge(y_s, n - SLOTS + 1)
                    sp.wait_ge(jxT_ps, n - SLOTS + 1)
                sp.wait_ge(st_xn[r], 16 * B)
                sp.dma_start(xg[:, r, :], xn_t[n]).then_inc(ld_xg[r], 16)
                sp.dma_start(x2[:, r, :], out_t[n]).then_inc(ld_x2[r], 16)

            def shared_store(q, r):
                n = num(q, r)
                sp.wait_ge(y_s, n + 1)
                sp.dma_start(out_t[n], y[:, r, :]).then_inc(st_y[r], 16)

            for r in range(SLOTS):
                shared_load(0, r)
            for r in range(SLOTS):
                shared_store(0, r)
                shared_load(1, r)
                if r < 3:
                    weights(B, r)
            with sp.Fori(1, J0 - 1) as q:
                for r in range(SLOTS):
                    shared_store(q, r)
                    shared_load(q + 1, r)
            for r in range(SLOTS):
                shared_store(J0 - 1, r)

        @block.gpsimd
        def _(pool):
            steps = [0]

            def then(ins):
                steps[0] += 1
                ins.then_inc(pool_step, 1)
                pool.wait_ge(pool_step, steps[0])

            g = nc.gpsimd
            then(g.memset(ident[:], 0.0))
            then(g.affine_select(out=ident[:], in_=ident[:], compare_op=ALU.not_equal, fill=1.0, base=0,
                                 pattern=[[-1, P]], channel_multiplier=1))
            g.memset(ones[:], 1.0)
            g.memset(mhalf[:], -0.5).then_inc(c_pool, 1)
            zeros = xT[:].rearrange("p s k t -> p (s k t)")[:, 0:D]
            then(g.memset(zeros, 0.0))
            g.dma_start(out_t[TILES], zeros).then_inc(st_trash, 16)
            pool.wait_ge(pen_ready0, 2)

            def penalty(q, r):
                if not (isinstance(q, int) and q == 0):
                    pool.wait_ge(max_s, before(pool, num(q, r) - SLOTS + 1))
                g.tensor_tensor(pen[:, r, :], mask_pen[:, r, :], kpad_pen[:, q, :], ALU.add).then_inc(pen_s, 1)

            def inv_std(q, r, stat_s, mv, ve, ve_s, rstd, rstd_s):
                t = num(q, r)
                pool.wait_ge(stat_s, before(pool, t + 1))
                g.tensor_scalar(ve[:, r:r + 1], mv[:, r, 1:2], EPS, None, ALU.add).then_inc(ve_s, 1)
                pool.wait_ge(ve_s, before(pool, t + 1))
                g.tensor_tensor(rstd[:, r:r + 1], ve[:, r:r + 1], mhalf[:], ALU.pow).then_inc(rstd_s, 1)

            def low_part(place, i, c):
                pool.wait_ge(hi_s, before(pool, c + 1))
                g.tensor_tensor(third((gu_lo, dn_lo), place, i), stage[:, i],
                                third((gu_hi, dn_hi), place, i).bitcast(f32), ALU.subtract).then_inc(lo_s, 1)

            def step(q, r):
                fixed = isinstance(q, int)
                if not (fixed and num(q, r) + 1 >= TILES):
                    nq, nr = shift(q, r, 1)
                    inv_std(nq, nr, xstat, mv1, ve1, ve1_s, rstd1, rstd1_s)
                if not (fixed and num(q, r) == 0):
                    pq, pr = shift(q, r, -1)
                    inv_std(pq, pr, mv2_s, mv2, ve2, ve2_s, rstd2, rstd2_s)
                if r > 0:
                    low_part(q, r - 1, chunk_number(q - 1, r - 1))
                if not (fixed and num(q, r) + 2 >= TILES):
                    penalty(*shift(q, r, 2))

            inv_std(0, 0, xstat, mv1, ve1, ve1_s, rstd1, rstd1_s)
            penalty(0, 0)
            penalty(0, 1)
            for r in range(RT):
                step(0, r)
            with pool.Fori(1, B - 1) as b:
                for r in range(RT):
                    step(b, r)
            for r in range(RT):
                step(B - 1, r)
            inv_std(B - 1, RT - 1, mv2_s, mv2, ve2, ve2_s, rstd2, rstd2_s)

            def iota(dst, pattern, base_, mult):
                return g.iota(dst, pattern=pattern, base=base_, channel_multiplier=mult,
                              allow_small_or_imprecise_dtypes=True)
            pool.wait_ge(max_s, TILES)
            g.memset(jprob[:, 0:TILES], 1.0)
            g.memset(jexpert[:, 0:TILES], SHARED)
            iota(idx8, [[0, TILES], [-1, E]], E, 0).then_inc(first_table, 1)
            iota(k128, [[0, E], [P, TILES]], 0, 0)
            iota(a128[:], [[P, NG]], 1, 0)
            iota(tok1[:], [[0, K], [P, TILES]], 1, 1)
            iota(iota1[:], [[1, P]], 1, 0)
            iota(pidx[:], [[0, 1]], T + 1, 1)
            then(g.memset(triangle[:], 1.0))
            g.affine_select(out=triangle[:], in_=triangle[:], compare_op=ALU.is_gt, fill=0.0, base=0,
                            pattern=[[1, P]], channel_multiplier=-1).then_inc(consts_s, 1)

            for c in range(6):
                low_part(B + c // 3, c % 3, chunk_number(B - 1, c))

            pool.wait_ge(G_s, 1)
            pool.wait_ge(prob_s, 1)
            pool.wait_ge(lo_s, chunk_number(B, 2) + 1)
            then(g.tensor_tensor(R[:, :, 0], G[:, :, 0:ROUTED], G[:, :, 1:NG], ALU.subtract))
            then(g.tensor_tensor(R[:, :, 1], R[:, :, 0],
                                 prob[:].rearrange("p k t -> p (k t)").unsqueeze(2).to_broadcast([P, K * TILES, ROUTED]),
                                 ALU.mult))
            g.tensor_tensor(R[:, :, 0], R[:, :, 0],
                            tok1[:].rearrange("p k t -> p (k t)").unsqueeze(2).to_broadcast([P, K * TILES, ROUTED]),
                            ALU.mult).then_inc(R_s, 1)
            pool.wait_ge(table_s, 1)

            def gather(q, r):
                n = num(q, r)
                pool.wait_ge(jxT_ps, before(pool, n - SLOTS + 1))
                g.tensor_copy(gidx[:, r, :], jgather[:, bass.ds(n - TILES, 1)]).then_inc(gidx_s, 1)
                pool.wait_ge(gidx_s, before(pool, n - TILES + 1))
                g.indirect_dma_start(
                    out=xg[:, r, :], out_offset=None, in_=xn_dram,
                    in_offset=bass.IndirectOffsetOnAxis(ap=gidx[:, r, :], axis=0),
                    bounds_check=T - 1).then_inc(gt_xg[r], 16)

            def scatter(q, r, after_scatter=True):
                n = num(q, r)
                g.tensor_copy(sidx[:, r, :], jscatter[:, bass.ds(n - TILES, 1)]).then_inc(sidx_s, 1)
                pool.wait_ge(sidx_s, before(pool, n - TILES + 1))
                pool.wait_ge(y_s, before(pool, n + 1))
                if after_scatter:
                    pq, pr = shift(q, r, -1)
                    pool.wait_ge(add_y[pr], before(pool, 16 * (pq - J0 + 1)))
                g.indirect_dma_start(
                    out=out, out_offset=bass.IndirectOffsetOnAxis(ap=sidx[:, r, :], axis=0),
                    in_=y[:, r, :], in_offset=None, bounds_check=T + P - 1, compute_op=ALU.add).then_inc(add_y[r], 16)

            for r in range(SLOTS):
                gather(J0, r)
            for r in range(SLOTS):
                pool.wait_ge(st_y[r], 16 * J0)
            pool.wait_ge(st_trash, 16)
            QL = ROUTED // SLOTS
            for r in range(SLOTS):
                scatter(J0, r, after_scatter=(r > 0))
                gather(J0 + 1, r)
            with pool.Fori(J0 + 1, J0 + QL - 1) as q:
                for r in range(SLOTS):
                    scatter(q, r)
                    gather(q + 1, r)
            for r in range(SLOTS):
                scatter(J0 + QL - 1, r)
                if r < ROUTED % SLOTS:
                    gather(J0 + QL, r)
            for r in range(ROUTED % SLOTS):
                scatter(J0 + QL, r)
            for r in range(SLOTS):
                pool.wait_ge(add_y[r], 16 * (QL + (1 if r < ROUTED % SLOTS else 0)))

        @block.scalar
        def _(act):
            a = nc.scalar
            act.dma_start(mask_in[:], mask.rearrange("(r p) s -> p r s", p=P)).then_inc(ld_mask, 16)
            act.dma_start(kpad_in[:].rearrange("p b s -> p (b s)"),
                          kpad.rearrange("b s -> (b s)").partition_broadcast(P)).then_inc(ld_mask, 16)
            act.wait_ge(ld_small, 64)
            a.mul(bqk[:, 0:1], bqk[:, 0:1], SCALING).then_inc(bq_ready, 1)
            act.wait_ge(wT_ps, 1)
            a.copy(wqkT[:].rearrange("p w o -> p (w o)"), ps_proj[0][:, 0:2 * H]).then_inc(wT_ready, 1)
            act.wait_ge(bq_ready, 1)

            def ctx_copy(b):
                act.wait_ge(ctxT_ps, b + 1)
                if b >= 2:
                    act.wait_ge(proj_ps, 2 * (b - 1))
                a.copy(ctxT[:, b % 2, :], ps_ctxT[:]).then_inc(ctxT_ready, 1)

            def projections(b):
                for w, dst in enumerate((qT, kT)):
                    act.wait_ge(proj_ps, 2 * b + w + 1)
                    a.activation(dst[:, b * S:(b + 1) * S], ps_proj[w][:], ACT.Identity, bias=bqk[:, w:w + 1],
                                 scale=SCALING if w == 0 else 1.0).then_inc(proj_ready, 1)

            def q_copy(q, r):
                t = num(q, r)
                if not (isinstance(q, int) and q == 0):
                    act.wait_ge(score_ps, t - SLOTS + 1)
                a.copy(q_tile[:, r, :], qT[:, bass.ds(P * t, P)]).then_inc(q_ready, 1)

            def expo(q, r):
                t = num(q, r)
                act.wait_ge(nbias_s, t + 1)
                a.activation(sc[:, r, :], sc[:, r, :], ACT.Exp, bias=nbias[:, r:r + 1], scale=rstd1[:, r:r + 1],
                             accum_out=rowsum[:, r:r + 1]).then_inc(exp_s, 1)

            def xnT_copy(q, r):
                t = num(q, r)
                act.wait_ge(xnT_ps, t + 1)
                a.copy(xT[:, r % 2].rearrange("p k t -> p (k t)"), ps_xnT[r % 2][:]).then_inc(xnT_ready, 1)

            def high_part(place, i, c, visit):
                act.wait_ge(ld_st[i], 32 * (visit + 1))
                a.copy(third((gu_hi, dn_hi), place, i), stage[:, i]).then_inc(hi_s, 1)

            def step(q, r, drop_q=False, project=None):
                expo(q, r)
                if project is not None:
                    projections(project)
                if not drop_q:
                    q_copy(*shift(q, r, 2))
                if project is not None and project + 1 < B:
                    ctx_copy(project + 1)
                if r < 3:
                    high_part(q, r, chunk_number(q - 1, r), q)
                tq, tr = shift(q, r, -2)
                if not early(tq):
                    xnT_copy(tq, tr)

            ctx_copy(0)
            projections(0)
            act.wait_ge(st_trash, 16)
            act.wait_ge(proj_ready, 2)
            q_copy(0, 0)
            q_copy(0, 1)
            ctx_copy(1)
            for t in range(HEAD):
                if t in (2, 3):
                    act.wait_ge(proj_ready, 4 if t == 2 else 2 * B)
                step(t // RT, t % RT, project=t + 1 if t + 1 < B else None)
            with act.Fori(1, LOOP_END) as b:
                for d in range(RT):
                    step(*shift(b, LAG, d))
            for t in range(TILES - LAG, TILES):
                step(t // RT, t % RT, drop_q=True)
            xnT_copy(B - 1, RT - 2)
            xnT_copy(B - 1, RT - 1)
            act.wait_ge(logit_ps, TILES)
            a.copy(lg[:].rearrange("p t e -> p (t e)"), ps_logit[:, 0:TILES * E]).then_inc(lg_s, 1)

            def x_high(q, r):
                n = num(q, r)
                act.wait_ge(jxT_ps, n + 1)
                if not (isinstance(q, int) and n < 2):
                    act.wait_ge(g_ps, n - 1)
                bank_ = ps_xT[r % 2][:].rearrange("p (k t) -> p k t", k=KC)
                a.copy(x_hi[:, r % 2], bank_).then_inc(xhi_s, 1)
                a.copy(x_bf[:, r % 2], bank_).then_inc(xbf_s, 1)

            def h_high(q, r):
                n = num(q, r)
                act.wait_ge(hT_ps, n + 1)
                if not (isinstance(q, int) and n < 2):
                    act.wait_ge(y_ps, n - 1)
                bank_ = ps_hT[:, 0:I].rearrange("p (c t) -> p c t", c=IC)
                a.copy(h_hi[:, r % 2], bank_).then_inc(hhi_s, 1)
                a.copy(h_bf[:, r % 2], bank_).then_inc(hbf_s, 1)

            def silu(q, r):
                n = num(q, r)
                act.wait_ge(g_ps, n + 1)
                if not (isinstance(q, int) and n < 2):
                    act.wait_ge(hT_ps, n - 1)
                a.activation(h[:, r % 2, :], ps_g[r % 2][:, 0:I], ACT.Silu,
                             scale=jprob[:, bass.ds(n, 1)]).then_inc(silu_s, 1)

            def job_step(q, r, last=False):
                pq, pr = shift(q, r, -1)
                if not early(pq):
                    h_high(pq, pr)
                silu(q, r)
                if not last:
                    x_high(*shift(q, r, 1))

            act.wait_ge(first_table, 1)
            for r in range(SLOTS):
                act.wait_ge(st_xn[r], 16 * B)
            act.wait_ge(logit_ps, TILES)
            x_high(0, 0)
            act.wait_ge(top_s, 1)
            a.activation(pexp[:], top[:], ACT.Exp, scale=-1.0).then_inc(pexp_s, 1)
            for n in range(10):
                if n == 2:
                    act.wait_ge(rank_ps, 1)
                    a.copy(rank.rearrange("p a t e -> p (a t e)"), ps_rank[:, 0:2 * TILES * E]).then_inc(rank_s, 1)
                job_step(n // SLOTS, n % SLOTS)
                if n < 6:
                    high_part(B + n // 3, n % 3, chunk_number(B - 1, n), B + n // 3)
            act.wait_ge(map_ps, 1)
            a.copy(amap[:].rearrange("p a j -> p (a j)"), ps_map[:, 0:2 * ROUTED]).then_inc(map_s, 1)
            for i in range(3):
                stage_weights(act, B + 1, i)
            for n in range(10, TILES):
                if n == TILES - 1:
                    act.wait_ge(table_s, 1)
                job_step(n // SLOTS, n % SLOTS)
                for c in range(2 * (n - 10), min(2 * (n - 10) + 2, 3 * LN)):
                    e, i = B + 1 + c // 3, c % 3
                    high_part(e + 1, i, chunk_number(e, i), e + 1)
                for c in range(2 * (n - 10) + 3, min(2 * (n - 10) + 5, 3 * LN)):
                    stage_weights(act, B + 1 + c // 3, c % 3)
            QF = JOBS // SLOTS
            with act.Fori(J0, QF) as q:
                for r in range(SLOTS):
                    job_step(q, r)
            for r in range(JOBS % SLOTS):
                job_step(QF, r, last=(r == JOBS % SLOTS - 1))
            h_high(QF, JOBS % SLOTS - 1)

        @block.vector
        def _(dve):
            v = nc.vector

            def x_stats(q, r):
                dve.wait_ge(ld_x[r], 16 * (q + 1))
                v.bn_stats(bn1[:, r, :], xin[:, r, :]).then_inc(bn1_s, 1)

            def x2_stats(q, r):
                dve.wait_ge(x2_s, num(q, r) + 1)
                v.bn_stats(bn2[:, r, :], x2[:, r, :]).then_inc(bn2_s, 1)

            def aggregate(q, r, bn, bn_s, mv, mv_s):
                dve.wait_ge(bn_s, before(dve, num(q, r) + 1))
                v.bn_aggr(mv[:, r, :], bn[:, r, :]).then_inc(mv_s, 1)

            def raw_scores(q, r):
                t = num(q, r)
                dve.wait_ge(score_ps, t + 1)
                dve.wait_ge(xstat, t + 1)
                v.scalar_tensor_tensor(sc[:, r, :], xin[:, r, :], mv1[:, r, 0:1], ps_score[r % 2][:],
                                       ALU.subtract, ALU.mult).then_inc(raw_s, 1)

            def mask_and_max(q, r):
                t = num(q, r)
                dve.wait_ge(raw_s, before(dve, t + 1))
                dve.wait_ge(pen_s, before(dve, t + 1))
                v.tensor_tensor_reduce(out=sc[:, r, :], in0=sc[:, r, :], in1=pen[:, r, :], scale=1.0, scalar=-BIG,
                                       op0=ALU.add, op1=ALU.max, accum_out=rowmax[:, r:r + 1]).then_inc(max_s, 1)

            def neg_max(q, r):
                t = num(q, r)
                dve.wait_ge(max_s, t + 1)
                dve.wait_ge(rstd1_s, t + 1)
                v.scalar_tensor_tensor(nbias[:, r:r + 1], rowmax[:, r:r + 1], -1.0, rstd1[:, r:r + 1],
                                       ALU.mult, ALU.mult).then_inc(nbias_s, 1)

            def kept_sum(q, r):
                dve.wait_ge(exp_s, num(q, r) + 1)
                v.scalar_tensor_tensor(rowsum[:, r:r + 1], rowmax[:, r:r + 1], MASKED / 2, rowsum[:, r:r + 1],
                                       ALU.is_gt, ALU.mult).then_inc(rsum_s, 1)

            def inv_sum(q, r):
                dve.wait_ge(rsum_s, num(q, r) + 1)
                v.reciprocal(rinv[:, r:r + 1], rowsum[:, r:r + 1]).then_inc(rinv_s, 1)

            def residual(q, r):
                dve.wait_ge(rinv_s, num(q, r) + 1)
                if not (isinstance(q, int) and q == 0):
                    dve.wait_ge(st_x2[r], 16 * q)
                v.scalar_tensor_tensor(x2[:, r, :], sc[:, r, :], rinv[:, r:r + 1], xin[:, r, :],
                                       ALU.mult, ALU.add).then_inc(x2_s, 1)

            def normal(q, r):
                t = num(q, r)
                dve.wait_ge(rstd2_s, t + 1)
                if not (isinstance(q, int) and q == 0):
                    dve.wait_ge(st_xn[r], 16 * q)
                    dve.wait_ge(xnT_ps, t - SLOTS + 1)
                v.tensor_scalar(xn[:, r, :], x2[:, r, :], mv2[:, r, 0:1], rstd2[:, r:r + 1],
                                ALU.subtract, ALU.mult).then_inc(xn_s, 1)

            def step(q, r, last=False):
                one, two = shift(q, r, -1), shift(q, r, -2)
                lag1, lag2 = not early(one[0]), not early(two[0])
                raw_scores(q, r)
                if lag1:
                    kept_sum(*one)
                mask_and_max(q, r)
                if lag1:
                    inv_sum(*one)
                neg_max(q, r)
                if lag1:
                    residual(*one)
                if not last:
                    x_stats(*shift(q, r, 1))
                if lag1:
                    x2_stats(*one)
                if not last:
                    aggregate(*shift(q, r, 1), bn1, bn1_s, mv1, xstat)
                if lag2:
                    normal(*two)
                if lag1:
                    aggregate(*one, bn2, bn2_s, mv2, mv2_s)

            dve.wait_ge(ld_mask, 32)
            v.tensor_scalar(mask_pen, mask_in[:], MASKED, None, ALU.mult).then_inc(pen_ready0, 1)
            v.tensor_scalar(kpad_pen, kpad_in[:], MASKED, None, ALU.mult).then_inc(pen_ready0, 1)
            x_stats(0, 0)
            aggregate(0, 0, bn1, bn1_s, mv1, xstat)
            for t in range(HEAD):
                step(t // RT, t % RT)
            with dve.Fori(1, LOOP_END) as b:
                for d in range(RT):
                    step(*shift(b, LAG, d))
            for t in range(TILES - LAG, TILES):
                step(t // RT, t % RT, last=(t == TILES - 1))
            kept_sum(B - 1, RT - 1)
            inv_sum(B - 1, RT - 1)
            residual(B - 1, RT - 1)
            normal(B - 1, RT - 2)
            x2_stats(B - 1, RT - 1)
            aggregate(B - 1, RT - 1, bn2, bn2_s, mv2, mv2_s)
            normal(B - 1, RT - 1)

            steps = [0]

            def then(ins):
                steps[0] += 1
                ins.then_inc(dve_step, 1)
                dve.wait_ge(dve_step, steps[0])

            def wide(column, shape):
                return column.unsqueeze(2).to_broadcast(shape)

            def choose():
                dve.wait_ge(first_table, 1)
                dve.wait_ge(lg_s, 1)
                src = lg[:]
                for k in range(K):
                    then(v.tensor_reduce(top[:, k], src, X, ALU.max))
                    then(v.tensor_tensor(eq, src, wide(top[:, k], [P, TILES, E]), ALU.is_equal))
                    then(v.tensor_tensor(eq, eq, idx8, ALU.mult))
                    then(v.tensor_reduce(best[:], eq, X, ALU.max))
                    then(v.tensor_tensor(oh[:, k], idx8, wide(best[:], [P, TILES, E]), ALU.is_equal))
                    if k == 0:
                        then(v.scalar_tensor_tensor(lg2, oh[:, 0], -BIG, lg[:], ALU.mult, ALU.add))
                        src = lg2
                v.tensor_scalar(top[:], top[:], -88.0, BIG, ALU.max, ALU.min).then_inc(top_s, 1)
                v.tensor_tensor(ohs[:], oh[:, 0], oh[:, 1], ALU.add).then_inc(oh_s, 1)

            def count():
                dve.wait_ge(consts_s, 1)
                dve.wait_ge(rank_s, 1)
                dve.wait_ge(pexp_s, 1)
                then(v.tensor_scalar(prob[:], pexp[:], 1.0, None, ALU.add))
                v.reciprocal(prob[:], prob[:]).then_inc(prob_s, 1)
                v.tensor_reduce(cnt[:], rank[:, 1].rearrange("p t e -> p e t"), X, ALU.add)
                then(v.tensor_copy(cum[:, 0], rank[:, 1]))
                then(v.tensor_tensor(cmp, wide(cnt[:], [P, E, TILES]), k128, ALU.is_gt))
                then(v.tensor_reduce(ntile[:, 0], cmp, X, ALU.add))
                for i, d in enumerate((1, 2, 4)):
                    v.tensor_copy(ntile[:, i + 1, 0:d], ntile[:, i, 0:d])
                    then(v.tensor_tensor(ntile[:, i + 1, d:], ntile[:, i, d:], ntile[:, i, 0:E - d], ALU.add))
                then(v.tensor_tensor(base[:], ntile[:, 3], ntile[:, 0], ALU.subtract))

            def places():
                side = 0
                for d in (1, 2, 4, 8):
                    v.tensor_copy(cum[:, 1 - side, 0:d], cum[:, side, 0:d])
                    then(v.tensor_tensor(cum[:, 1 - side, d:], cum[:, side, d:], cum[:, side, 0:TILES - d], ALU.add))
                    side = 1 - side
                then(v.tensor_tensor(place, cum[:, side], rank[:, 1], ALU.subtract))
                then(v.tensor_scalar(base[:], base[:], float(P), 1.0, ALU.mult, ALU.add))
                then(v.tensor_tensor(place, place, rank[:, 0], ALU.add))
                then(v.tensor_tensor(place, place, base[:].unsqueeze(1).to_broadcast([P, TILES, E]), ALU.add))
                for k in range(K):
                    then(v.tensor_tensor(eq, oh[:, k], place, ALU.mult))
                    then(v.tensor_reduce(slot1[:, k], eq, X, ALU.add))

            slots = slot1[:].rearrange("p k t -> p (k t)")

            def job_of_choice():
                then(v.tensor_tensor(G, wide(slots, [P, K * TILES, NG]),
                                     a128[:].unsqueeze(1).to_broadcast([P, K * TILES, NG]), ALU.is_ge))
                v.tensor_reduce(acol[:], G[:, :, 1:NG], X, ALU.add).then_inc(G_s, 1)
                dve.wait_ge(G_s, 1)
                then(v.scalar_tensor_tensor(bcol[:], acol[:], -float(P), slots, ALU.mult, ALU.add))

            def row_of_choice(half):
                c0, c1 = half * TILES, (half + 1) * TILES
                v.tensor_tensor(OB[:, c0:c1], iota1[:].unsqueeze(1).to_broadcast([P, TILES, P]),
                                wide(bcol[:, c0:c1], [P, TILES, P]), ALU.is_equal).then_inc(OB_s, 1)

            def job_experts():
                then(v.tensor_scalar(ntile[:, 0], ntile[:, 3], float(P), 1.0, ALU.mult, ALU.add))
                then(v.tensor_tensor(ecmp[:], wide(a128[:, 0:ROUTED], [P, ROUTED, E]),
                                     ntile[:, 0].unsqueeze(1).to_broadcast([P, ROUTED, E]), ALU.is_ge))
                then(v.tensor_reduce(efl[:], ecmp[:], X, ALU.add))
                v.tensor_scalar(jexpert[:, TILES:JOBS], efl[:], float(E - 1), 1.0, ALU.min, ALU.add)

            def tables():
                dve.wait_ge(map_s, 1)
                then(v.tensor_scalar(hole[:], amap[:, 0], 0.0, None, ALU.is_equal))
                v.tensor_scalar(jgather[:], amap[:, 0], -1.0, 0.0, ALU.add, ALU.max)
                then(v.scalar_tensor_tensor(jf[:], hole[:], pidx[:], amap[:, 0], ALU.mult, ALU.add))
                v.tensor_copy(jprob[:, TILES:JOBS], amap[:, 1])
                v.tensor_scalar(jscatter[:], jf[:], -1.0, None, ALU.add).then_inc(table_s, 1)

            def h_low(q, r):
                n = num(q, r)
                dve.wait_ge(hbf_s, n + 1)
                if not (isinstance(q, int) and n < 2):
                    dve.wait_ge(y_ps, n - 1)
                v.tensor_tensor(h_lo[:, r % 2], ps_hT[:, 0:I].rearrange("p (c t) -> p c t", c=IC),
                                h_hi[:, r % 2].bitcast(f32), ALU.subtract).then_inc(hlo_s, 1)

            def x_low(q, r):
                n = num(q, r)
                dve.wait_ge(xbf_s, n + 1)
                if not (isinstance(q, int) and n < 2):
                    dve.wait_ge(g_ps, n - 1)
                v.tensor_tensor(x_lo[:, r % 2], ps_xT[r % 2][:].rearrange("p (k t) -> p k t", k=KC),
                                x_hi[:, r % 2].bitcast(f32), ALU.subtract).then_inc(xlo_s, 1)

            def low_part(expert, i):
                dve.wait_ge(hi_s, chunk_number(expert, i) + 1)
                v.tensor_tensor(third((gu_lo, dn_lo), expert + 1, i), stage[:, i],
                                third((gu_hi, dn_hi), expert + 1, i).bitcast(f32), ALU.subtract).then_inc(lo_s, 1)

            def gated(q, r):
                n = num(q, r)
                if isinstance(q, int) and n == TILES:
                    dve.wait_ge(table_s, 1)
                dve.wait_ge(silu_s, n + 1)
                v.scalar_tensor_tensor(h[:, r % 2, :], ps_g[r % 2][:, I:2 * I], jprob[:, bass.ds(n, 1)],
                                       h[:, r % 2, :], ALU.mult, ALU.mult).then_inc(h_s, 1)

            def y_out(q, r, shared):
                n = num(q, r)
                dve.wait_ge(y_ps, n + 1)
                if isinstance(q, int) and 0 < q <= J0:
                    dve.wait_ge(st_y[r], 16 * q)
                elif not isinstance(q, int) or q > J0:
                    dve.wait_ge(add_y[r], 16 * (q - J0))
                if shared:
                    dve.wait_ge(ld_x2[r], 16 * (q + 1))
                    v.tensor_tensor(y[:, r, :], ps_y[r % 2][:], x2[:, r, :], ALU.add).then_inc(y_s, 1)
                else:
                    v.tensor_copy(y[:, r, :], ps_y[r % 2][:]).then_inc(y_s, 1)

            def job_step(q, r, shared=False, last=False):
                pq, pr = shift(q, r, -1)
                if not early(pq):
                    h_low(pq, pr)
                gated(q, r)
                if not last:
                    x_low(*shift(q, r, 1))
                if not early(pq):
                    y_out(pq, pr, shared)

            for r in range(SLOTS):
                dve.wait_ge(st_xn[r], 16 * B)
            x_low(0, 0)
            choose()
            for r in range(3):
                job_step(0, r, shared=True)
            count()
            job_step(0, 3, shared=True)
            places()
            job_step(1, 0, shared=True)
            job_of_choice()
            job_step(1, 1, shared=True)
            row_of_choice(0)
            job_step(1, 2, shared=True)
            row_of_choice(1)
            job_step(1, 3, shared=True)
            job_experts()
            for n in range(8, 11):
                job_step(n // SLOTS, n % SLOTS, shared=True)
            tables()
            for n in range(11, TILES + 1):
                c0 = 2 * (n - 11)
                for c in range(c0, min(c0 + 2, 3 * LN)):
                    low_part(B + 1 + c // 3, c % 3)
                job_step(n // SLOTS, n % SLOTS, shared=True)
            QF = JOBS // SLOTS
            for r in range(1, SLOTS):
                job_step(J0, r)
            with dve.Fori(J0 + 1, QF) as q:
                for r in range(SLOTS):
                    job_step(q, r)
            for r in range(JOBS % SLOTS):
                job_step(QF, r, last=(r == JOBS % SLOTS - 1))
            lq, lr = QF, JOBS % SLOTS - 1
            h_low(lq, lr)
            y_out(lq, lr, False)

        @block.tensor
        def _(pe):
            tn = nc.tensor
            pe.wait_ge(c_pool, 1)
            pe.wait_ge(ld_small, 64)
            for w in range(2):
                last = tn.transpose(ps_proj[0][:, w * H:(w + 1) * H], wqk[:, w, :], ident[:])
            last.then_inc(wT_ps, 1)

            def ctx_transpose(b):
                pe.wait_ge(ld_ctx if b else ld_ctx0, 16)
                if b:
                    pe.wait_ge(ctxT_ready, b)
                for r in range(RT):
                    last = tn.transpose(ps_ctxT[:, r * P:(r + 1) * P], ctx_in[:, b * RT + r, :], ident[:])
                last.then_inc(ctxT_ps, 1)

            def projections(b):
                if b == 0:
                    pe.wait_ge(wT_ready, 1)
                pe.wait_ge(ctxT_ready, b + 1)
                for w in range(2):
                    if b:
                        pe.wait_ge(proj_ready, 2 * b - 1 + w)
                    tn.matmul(ps_proj[w][:], wqkT[:, w, :], ctxT[:, b % 2, :], start=True, stop=True).then_inc(proj_ps, 1)

            def scores(q, r):
                t = num(q, r)
                pe.wait_ge(q_ready, t + 1)
                if not (isinstance(q, int) and num(q, r) < 2):
                    pe.wait_ge(raw_s, t - 1)
                tn.matmul(ps_score[r % 2][:], q_tile[:, r, :], kT[:, bass.ds(S * q, S)], start=True,
                          stop=True).then_inc(score_ps, 1)

            def xn_transpose(q, r):
                t = num(q, r)
                pe.wait_ge(xn_s, t + 1)
                if not (isinstance(q, int) and num(q, r) < 2):
                    pe.wait_ge(xnT_ready, t - 1)
                for k in range(KC):
                    last = tn.transpose(ps_xnT[r % 2][:, k * P:(k + 1) * P], xn[:, r, k * P:(k + 1) * P], ident[:])
                last.then_inc(xnT_ps, 1)

            def logits(q, r):
                t = num(q, r)
                pe.wait_ge(xnT_ready, t + 1)
                for k in range(KC):
                    last = tn.matmul(ps_logit[:, bass.ds(E * t, E)], xT[:, r % 2, k, :], rw[:, k, :],
                                     start=(k == 0), stop=(k == KC - 1))
                last.then_inc(logit_ps, 1)

            def step(q, r, last=False, project=None):
                if project is not None:
                    projections(project)
                if not last:
                    scores(*shift(q, r, 2))
                if project is not None and project + 1 < B:
                    ctx_transpose(project + 1)
                pq, pr = shift(q, r, -2)
                if not early(pq):
                    xn_transpose(pq, pr)
                pq, pr = shift(q, r, -3)
                if not early(pq):
                    logits(pq, pr)

            ctx_transpose(0)
            projections(0)
            ctx_transpose(1)
            pe.wait_ge(proj_ready, 2)
            scores(0, 0)
            scores(0, 1)
            pe.wait_ge(ld_rw, 16)
            for t in range(HEAD):
                if t in (2, 3):
                    pe.wait_ge(proj_ready, 4 if t == 2 else 2 * B)
                step(t // RT, t % RT, project=t + 1 if t + 1 < B else None)
            with pe.Fori(1, LOOP_END) as b:
                for d in range(RT):
                    step(*shift(b, LAG, d))
            for t in range(TILES - LAG, TILES):
                step(t // RT, t % RT, last=True)
            for r in (RT - 2, RT - 1):
                xn_transpose(B - 1, r)
                logits(B - 1, r - 1)
            logits(B - 1, RT - 1)

            def x_transpose(q, r):
                n = num(q, r)
                if isinstance(q, int) and q < J0:
                    pe.wait_ge(ld_xg[r], 16 * (q + 1))
                else:
                    pe.wait_ge(gt_xg[r], 16 * (q - J0 + 1))
                if not (isinstance(q, int) and num(q, r) < 2):
                    pe.wait_ge(xlo_s, n - 1)
                for k in range(KC):
                    last = tn.transpose(ps_xT[r % 2][:, k * P:(k + 1) * P], xg[:, r, k * P:(k + 1) * P], ident[:])
                last.then_inc(jxT_ps, 1)

            def expert(n):
                return pe.value_load(jexpert[0:1, bass.ds(n, 1)], min_val=0, max_val=E)

            def gate_up(q, r, e):
                n = num(q, r)
                pe.wait_ge(xhi_s, n + 1)
                if not (isinstance(q, int) and num(q, r) < 2):
                    pe.wait_ge(h_s, n - 1)
                for k in range(KC):
                    tn.matmul(ps_g[r % 2][:], x_hi[:, r % 2, k, :], gu_hi[:, e, k, :], start=(k == 0), stop=False)
                pe.wait_ge(xbf_s, n + 1)
                for k in range(KC):
                    tn.matmul(ps_g[r % 2][:], x_bf[:, r % 2, k, :], gu_lo[:, e, k, :], start=False, stop=False)
                pe.wait_ge(xlo_s, n + 1)
                for k in range(KC):
                    last = tn.matmul(ps_g[r % 2][:], x_lo[:, r % 2, k, :], gu_hi[:, e, k, :], start=False,
                                     stop=(k == KC - 1))
                last.then_inc(g_ps, 1)

            def h_transpose(q, r):
                n = num(q, r)
                pe.wait_ge(h_s, n + 1)
                if not (isinstance(q, int) and num(q, r) == 0):
                    pe.wait_ge(hlo_s, n)
                    pe.wait_ge(hbf_s, n)
                for c in range(IC):
                    last = tn.transpose(ps_hT[:, c * P:(c + 1) * P], h[:, r % 2, c * P:(c + 1) * P], ident[:])
                last.then_inc(hT_ps, 1)

            def down(q, r):
                n = num(q, r)
                e = expert(n)
                pe.wait_ge(hhi_s, n + 1)
                if not (isinstance(q, int) and num(q, r) < 2):
                    pe.wait_ge(y_s, n - 1)
                for c in range(IC):
                    tn.matmul(ps_y[r % 2][:], h_hi[:, r % 2, c, :], dn_hi[:, e, c, :], start=(c == 0), stop=False)
                pe.wait_ge(hbf_s, n + 1)
                for c in range(IC):
                    tn.matmul(ps_y[r % 2][:], h_bf[:, r % 2, c, :], dn_lo[:, e, c, :], start=False, stop=False)
                pe.wait_ge(hlo_s, n + 1)
                for c in range(IC):
                    last = tn.matmul(ps_y[r % 2][:], h_lo[:, r % 2, c, :], dn_hi[:, e, c, :], start=False,
                                     stop=(c == IC - 1))
                last.then_inc(y_ps, 1)

            def job_step(q, r, last=False):
                pq, pr = shift(q, r, -1)
                e = expert(num(q, r))
                if not early(pq):
                    h_transpose(pq, pr)
                gate_up(q, r, e)
                if not last:
                    x_transpose(*shift(q, r, 1))
                if not early(pq):
                    down(pq, pr)

            pe.wait_ge(first_table, 1)
            pe.wait_ge(raw_s, TILES)
            x_transpose(0, 0)
            pe.wait_ge(lo_s, 3)
            job_step(0, 0)
            job_step(0, 1)
            pe.wait_ge(consts_s, 1)
            pe.wait_ge(oh_s, 1)
            tn.matmul(ps_rank[:, 0:TILES * E], triangle[:], ohs[:].rearrange("p t e -> p (t e)"), start=True, stop=True)
            tn.matmul(ps_rank[:, TILES * E:2 * TILES * E], ones[:], ohs[:].rearrange("p t e -> p (t e)"),
                      start=True, stop=True).then_inc(rank_ps, 1)
            for n in range(2, 10):
                job_step(n // SLOTS, n % SLOTS)
            pe.wait_ge(R_s, 1)
            pe.wait_ge(OB_s, 2)
            for i in range(K * TILES):
                last = tn.matmul(ps_map[:, 0:2 * ROUTED], OB[:, i, :], R[:, i].rearrange("p a j -> p (a j)"),
                                 start=(i == 0), stop=(i == K * TILES - 1))
            last.then_inc(map_ps, 1)
            for n in range(10, TILES):
                if n == TILES - 1:
                    pe.wait_ge(table_s, 1)
                job_step(n // SLOTS, n % SLOTS)
            pe.wait_ge(lo_s, 3 * (E + 1))
            QF = JOBS // SLOTS
            with pe.Fori(TILES // SLOTS, QF) as q:
                for r in range(SLOTS):
                    job_step(q, r)
            for r in range(JOBS % SLOTS):
                job_step(QF, r, last=(r == JOBS % SLOTS - 1))
            h_transpose(QF, JOBS % SLOTS - 1)
            down(QF, JOBS % SLOTS - 1)


_INS = ['x', 'ctx_512', 'mask_SxS2_bk1', 'mask_BxS2_bf0', 'L0_xattn_Wq', 'L0_xattn_bq', 'L0_xattn_Wk',
        'L0_xattn_bk', 'L0_ffn_router_w', 'L0_ffn_gate_up_w', 'L0_ffn_down_w', 'L0_ffn_shared_gate_w',
        'L0_ffn_shared_up_w', 'L0_ffn_shared_down_w']


def kernel(**inputs):
    import concourse.bacc as _bacc
    from concourse.bass_utils import run_bass_kernel_spmd as _run

    nc = _bacc.Bacc("TRN2", target_bir_lowering=False, num_devices=1, dynamic_dma_scratch_size=SCRATCH)
    arrays, args = {}, []
    for name in _INS:
        a = np.ascontiguousarray(inputs[name])
        arrays[f"in_{name}"] = a
        args.append(nc.dram_tensor(f"in_{name}", a.shape, mybir.dt.from_np(a.dtype), kind="ExternalInput").ap())
    args.append(nc.dram_tensor("out_rows", (T + P, D), mybir.dt.float32, kind="ExternalOutput").ap())
    build(nc, *args)
    r = _run(nc, [arrays], core_ids=[0])
    return r.results[0]["out_rows"][:T].reshape(B, S, D)
```

```python
import numpy as np
import concourse.bass as bass
from concourse import mybir
from contextlib import ExitStack

P = 128
B, S, D, H = 4, 512, 512, 128
T = B * S
TILES = T // P
RT = S // P
KC = D // P
E, K, I = 8, 2, 256
IC = I // P
SHARED = 0
LATE = E // 2 + 2
CH = 2
ROUTED = (K * T + E * (P - 1)) // P
JOBS = TILES + ROUTED
EPS = 1e-5
SCALING = float(H) ** -0.5
BIG = 3e38
MASKED = -1e30
LAG = 2
HEAD = RT + LAG
LOOP_END = B - 1
SCRATCH = 2048
SLOTS = 4


def build(nc, x, ctx, mask, kpad, wq, bq, wk, bk, router_w, gate_up_w, down_w, sg_w, su_w, sd_w, out):
    f32r = mybir.dt.float32r
    f32, bf16, i32, u8 = mybir.dt.float32, mybir.dt.bfloat16, mybir.dt.int32, mybir.dt.uint8
    ALU, ACT, X = mybir.AluOpType, mybir.ActivationFunctionType, mybir.AxisListType.X

    x_t = x.rearrange("b (r p) d -> (b r) p d", p=P)
    out_t = out.rearrange("(t p) d -> t p d", p=P)
    xn_dram = nc.dram_tensor("xn_rows", (T, D), f32, kind="Internal").ap()
    xn_t = xn_dram.rearrange("(t p) d -> t p d", p=P)
    xnT_t = nc.dram_tensor("xn_transposed", (TILES, P, D), f32, kind="Internal").ap()

    stack = ExitStack()
    with stack:
        def sb(name, shape, dt=f32):
            return stack.enter_context(nc.sbuf_tensor(name, shape, dt))

        def sem(name):
            return stack.enter_context(nc.semaphore(name))

        def sems(name, n=SLOTS):
            return [sem(f"{name}{i}") for i in range(n)]

        LN = E + 1 - LATE
        under = ExitStack()

        def u(name, shape, dt=f32):
            return under.enter_context(nc.sbuf_tensor(name, shape, dt))

        u("gu_hi_head", [P, LATE, KC, 2 * I])
        qkT = u("qkT", [P, 2 * T])
        ctx_in = u("ctx_in", [P, TILES, H])
        u("dn_hi_head", [P, LATE, IC, D])
        ctxT = u("ctxT", [P, 2, S])
        mask_in = u("mask_in", [P, RT, S], u8)
        kpad_in = u("kpad_in", [P, B, S], u8)
        q_tile = u("q_tile", [P, SLOTS, P])
        u("dn_hi_rest", [P, LN * IC * D - 2 * S - (RT + B) * S // 4 - SLOTS * P])
        u("gu_lo_head", [P, LATE, KC, 2 * I], bf16)
        pens = u("pens", [P, RT + B + SLOTS, S], bf16)
        u("dn_lo_head", [P, LATE, IC, D], bf16)
        wqk = u("wqk", [P, 2, H])
        wqkT = u("wqkT", [P, 2, H])
        oh = u("oh", [P, K, TILES, E])
        ohs = u("ohs", [P, TILES, E])
        triangle = u("triangle", [P, P])
        iota1 = u("iota1", [P, P])
        u("dn_lo_rest", [P, LN * IC * D - 8 * H - 2 * K * TILES * E - 2 * TILES * E - 4 * P], bf16)
        xT = u("xT", [P, 2, KC, P])
        xn = u("xn", [P, SLOTS, D])
        under.close()
        gu_hi = sb("gu_hi", [P, E + 1, KC, 2 * I], f32r)
        dn_hi = sb("dn_hi", [P, E + 1, IC, D], f32r)
        gu_lo = sb("gu_lo", [P, E + 1, KC, 2 * I], bf16)
        dn_lo = sb("dn_lo", [P, E + 1, IC, D], bf16)
        x_hi = sb("x_hi", [P, 2, KC, P], f32r)
        x_lo = sb("x_lo", [P, 2, KC, P], f32r)
        h_lo = sb("h_lo", [P, 2, IC, P], f32r)
        x_bf = sb("x_bf", [P, 2, KC, P], bf16)
        mask_pen = pens[:, 0:RT]
        kpad_pen = pens[:, RT:RT + B]
        pen = pens[:, RT + B:]
        qT = qkT[:, 0:T]
        kT = qkT[:, T:2 * T]
        stage = sb("stage", [P, 3, CH, D])
        rw = sb("rw", [P, KC, E])
        bqk = sb("bqk", [P, 2])
        ident = sb("ident", [P, P])
        ones = sb("ones", [P, P])
        xin = sb("xin", [P, SLOTS, D])
        sc = sb("sc", [P, SLOTS, S])
        x2 = sb("x2", [P, SLOTS, D])
        bn1 = sb("bn1", [P, SLOTS, 6])
        mv1 = sb("mv1", [P, SLOTS, 2])
        bn2 = sb("bn2", [P, SLOTS, 6])
        mv2 = sb("mv2", [P, SLOTS, 2])
        ve1 = sb("ve1", [P, SLOTS])
        ve2 = sb("ve2", [P, SLOTS])
        rstd1 = sb("rstd1", [P, SLOTS])
        rstd2 = sb("rstd2", [P, SLOTS])
        rowmax = sb("rowmax", [P, SLOTS])
        nbias = sb("nbias", [P, SLOTS])
        rowsum = sb("rowsum", [P, SLOTS])
        rinv = sb("rinv", [P, SLOTS])
        mhalf = sb("mhalf", [P, 1])
        xg = sc
        y = xin
        h = sb("h", [P, 2, I])
        h_hi = sb("h_hi", [P, 2, IC, P], f32r)
        h_bf = sb("h_bf", [P, 2, IC, P], bf16)
        jprob = sb("jprob", [P, JOBS])
        jexpert = sb("jexpert", [P, JOBS], i32)
        jgather = sb("jgather", [P, ROUTED], i32)
        jscatter = sb("jscatter", [P, ROUTED], i32)
        gidx = sb("gidx", [P, SLOTS, 1], i32)
        sidx = sb("sidx", [P, SLOTS, 1], i32)
        NG = ROUTED + 1
        spare = [0]

        def old(name_, shape):
            n = int(np.prod(shape[1:]))
            at, spare[0] = spare[0], spare[0] + n
            letters = "abc"[:len(shape) - 1]
            return pens[:].rearrange("p r s -> p (r s)").bitcast(f32)[:, at:at + n].rearrange(
                f"p ({' '.join(letters)}) -> p {' '.join(letters)}", **dict(zip(letters[1:], shape[2:])))

        G = old("G", [P, K * TILES, NG])
        eq = old("eq", [P, TILES, E])
        key = old("key", [P, TILES, E])
        lg2 = old("lg2", [P, TILES, E])
        idx8 = old("idx8", [P, TILES, E])
        rank = old("rank", [P, 2, TILES, E])
        cum = old("cum", [P, 2, TILES, E])
        k128 = old("k128", [P, E, TILES])
        cmp = old("cmp", [P, E, TILES])
        place = old("place", [P, TILES, E])
        ecmp = old("ecmp", [P, ROUTED, E])
        lg = sb("lg", [P, TILES, E])
        top = sb("top", [P, K, TILES])
        best = sb("best", [P, TILES])
        prob = sb("prob", [P, K, TILES])
        pexp = sb("pexp", [P, K, TILES])
        cnt = sb("cnt", [P, E])
        ntile = sb("ntile", [P, 4, E])
        slot1 = sb("slot1", [P, K, TILES])
        base = sb("base", [P, E])
        a128 = sb("a128", [P, NG])
        acol = sb("acol", [P, K * TILES])
        bcol = sb("bcol", [P, K * TILES])
        tok1 = sb("tok1", [P, K, TILES])
        OB = qkT[:].rearrange("p (c j) -> p c j", j=P)
        R = stage[:].rearrange("p s c d -> p (s c d)")[:, 0:K * TILES * 2 * ROUTED].rearrange(
            "p (c m a) -> p c m a", m=2, a=ROUTED)
        efl = sb("efl", [P, ROUTED])
        amap = sb("amap", [P, 2, ROUTED])
        pidx = sb("pidx", [P, 1])
        hole = sb("hole", [P, ROUTED])
        jf = sb("jf", [P, ROUTED])

        bank = [stack.enter_context(nc.psum_tensor(f"bank{i}", [P, 512], f32)) for i in range(8)]
        ps_score = bank[0:2]
        ps_xnT = bank[2:4]
        ps_logit = bank[4]
        ps_ctxT = bank[7]
        ps_proj = bank[5:7]
        ps_g = bank[0:2]
        ps_xT = [bank[2], bank[7]]
        ps_hT = bank[3]
        ps_y = bank[5:7]
        ps_rank = bank[4]
        ps_map = bank[4]

        ld_ctx0 = sem("ld_ctx0")
        ld_ctx, ld_small, ld_mask, ld_rw = sem("ld_ctx"), sem("ld_small"), sem("ld_mask"), sem("ld_rw")
        ld_x, st_x2, st_xn = sems("ld_x"), sems("st_x2"), sems("st_xn")
        ld_xg, ld_x2, st_y = sems("ld_xg"), sems("ld_x2"), sems("st_y")
        gt_xg, add_y = sems("gt_xg"), sems("add_y")
        st_xnT = sems("st_xnT", 2)
        st_trash = sem("st_trash")
        ld_st = sems("ld_st", 3)
        hi_s, lo_s = sem("hi_s"), sem("lo_s")
        down_lo_s = sem("down_lo_s")
        c_pool = sem("c_pool")
        c_zero = sem("c_zero")
        pen_ready0 = sem("pen_ready0")
        wT_ps, wT_ready, ctxT_ps, ctxT_ready, proj_ps, proj_ready = (
            sem("wT_ps"), sem("wT_ready"), sem("ctxT_ps"), sem("ctxT_ready"), sem("proj_ps"), sem("proj_ready"))
        bq_ready = sem("bq_ready")
        q_ready, score_ps, xstat, bn1_s, bn2_s, ve1_s, ve2_s = (
            sem("q_ready"), sem("score_ps"), sem("xstat"), sem("bn1_s"), sem("bn2_s"), sem("ve1_s"), sem("ve2_s"))
        rstd1_s, rstd2_s, pen_s, raw_s, max_s, nbias_s, exp_s, rinv_s, x2_s, mv2_s, xn_s = (
            sem("rstd1_s"), sem("rstd2_s"), sem("pen_s"), sem("raw_s"), sem("max_s"), sem("nbias_s"), sem("exp_s"),
            sem("rinv_s"), sem("x2_s"), sem("mv2_s"), sem("xn_s"))
        xnT_ps, xnT_ready, logit_ps = sem("xnT_ps"), sem("xnT_ready"), sem("logit_ps")
        jxT_ps, xhi_s, xbf_s, xlo_s, g_ps, silu_s, h_s, hT_ps, hhi_s, hbf_s, hlo_s, y_ps, y_s = (
            sem("jxT_ps"), sem("xhi_s"), sem("xbf_s"), sem("xlo_s"), sem("g_ps"), sem("silu_s"), sem("h_s"),
            sem("hT_ps"), sem("hhi_s"), sem("hbf_s"), sem("hlo_s"), sem("y_ps"), sem("y_s"))
        lg_s, top_s, pexp_s, oh_s, rank_ps, rank_s, map_ps, map_s, table_s = (
            sem("lg_s"), sem("top_s"), sem("pexp_s"), sem("oh_s"), sem("rank_ps"), sem("rank_s"),
            sem("map_ps"), sem("map_s"), sem("table_s"))
        consts_s, prob_s, G_s, R_s, OB_s = sem("consts_s"), sem("prob_s"), sem("G_s"), sem("R_s"), sem("OB_s")
        rsum_s, rsraw_s = sem("rsum_s"), sem("rsraw_s")
        gidx_s, sidx_s = sem("gidx_s"), sem("sidx_s")
        pool_step, dve_step = sem("pool_step"), sem("dve_step")
        first_table = sem("first_table")

        block = stack.enter_context(nc.Block())

        def shift(q, r, by):
            return q + (r + by) // SLOTS, (r + by) % SLOTS

        def is_shared(q):
            return isinstance(q, int) and q < J0

        def rows_T(q, r):
            src = xg[:, r, :] if is_shared(q) else ps_xT[r % 2][:]
            return src.rearrange("p (k t) -> p k t", k=KC)

        def before(engine, value):
            if not isinstance(value, int):
                value = engine.snap(engine.to_reg(value))
                engine.wait_ge(c_pool, 1)
            return value

        def num(q, r):
            return SLOTS * q + r

        def stored_xnT(q, r):
            return 16 * (2 * q + r // 2 + 1)

        J0 = TILES // SLOTS

        def early(q):
            return isinstance(q, int) and q < 0

        def third(pair, place, i):
            return pair[0][:, place, CH * i:CH * (i + 1), :] if i < 2 else pair[1][:, place]

        gu_src = gate_up_w.rearrange("e (k p) f -> e p k f", p=P)
        dn_src = down_w.rearrange("e (k p) d -> e p k d", p=P)

        def chunk_number(expert, i):
            return 3 * (expert + 1) + i

        def stage_weights(engine, expert, i):
            c = chunk_number(expert, i)
            engine.wait_ge(hi_s, c - 2)
            before_it = c - 3 - FIRST_LATE if isinstance(c, int) else -1
            if before_it < 0:
                engine.wait_ge(lo_s, c - 2)
            elif i < 2:
                engine.wait_ge(lo_s, late_lo(before_it))
            else:
                engine.wait_ge(down_lo_s, before_it // 3 + 1)
            src = gu_src[expert, :, CH * i:CH * (i + 1), :] if i < 2 else dn_src[expert]
            for a in range(CH):
                engine.dma_start(stage[:, i, a, :], src[:, a, :]).then_inc(ld_st[i], 16)

        MAP_JOB = 10

        def late_chunks(n):
            return range(3 * ((n - MAP_JOB) // 2) + 2 * ((n - MAP_JOB) % 2), 3 * ((n - MAP_JOB) // 2) + 2 + (n - MAP_JOB) % 2)

        FIRST_LATE = 3 * (B + 2)

        def late_lo(c):
            return FIRST_LATE + 2 * (c // 3) + c % 3 + 1

        @block.sync
        def _(sp):
            ctx_rows = ctx.rearrange("b (r p) h -> p (b r) h", p=P)
            sp.dma_start(wqk[:, 0, :], wq).then_inc(ld_small, 16)
            sp.dma_start(wqk[:, 1, :], wk).then_inc(ld_small, 16)
            sp.dma_start(ctx_in[:, 0:RT], ctx_rows[:, 0:RT]).then_inc(ld_ctx0, 16)
            sp.dma_start(bqk[:, 0:1], bq.rearrange("(p o) -> p o", o=1)).then_inc(ld_small, 16)
            sp.dma_start(bqk[:, 1:2], bk.rearrange("(p o) -> p o", o=1)).then_inc(ld_small, 16)
            sp.dma_start(xin[:, 0, :], x_t[0]).then_inc(ld_x[0], 16)
            sp.dma_start(ctx_in[:, RT:], ctx_rows[:, RT:]).then_inc(ld_ctx, 16)
            sp.dma_start(xin[:, 1, :], x_t[1]).then_inc(ld_x[1], 16)
            sp.dma_start(rw[:], router_w.rearrange("(k p) e -> p k e", p=P)).then_inc(ld_rw, 16)
            for i in range(2):
                for half, w in enumerate((sg_w, su_w)):
                    sp.dma_start(stage[:, i, :, half * I:(half + 1) * I],
                                 w.rearrange("(k p) f -> p k f", p=P)[:, CH * i:CH * (i + 1), :]).then_inc(ld_st[i], 16)
            sp.dma_start(stage[:, 2, 0, :], sd_w.rearrange("(k p) d -> p k d", p=P)[:, 0, :]).then_inc(ld_st[2], 16)
            sp.dma_start(stage[:, 2, 1, :], sd_w.rearrange("(k p) d -> p k d", p=P)[:, 1, :]).then_inc(ld_st[2], 16)
            for r in range(2, SLOTS):
                sp.dma_start(xin[:, r, :], x_t[r]).then_inc(ld_x[r], 16)

            def weights(expert, i):
                stage_weights(sp, expert, i)

            def xnT_io(q, r):
                sp.wait_ge(xnT_ready, num(q, r) + 1)
                sp.dma_start(xnT_t[num(q, r)], xT[:, r % 2].rearrange("p k t -> p (k t)")).then_inc(st_xnT[r % 2], 16)

            def attention_io(q, r, last=False):
                t = num(q, r)
                sp.wait_ge(x2_s, t + 1)
                sp.dma_start(out_t[t], x2[:, r, :]).then_inc(st_x2[r], 16)
                if not last:
                    sp.dma_start(xin[:, r, :], x_t[t + SLOTS]).then_inc(ld_x[r], 16)
                sp.wait_ge(xn_s, t + 1)
                sp.dma_start(xn_t[t], xn[:, r, :]).then_inc(st_xn[r], 16)
                pq, pr = shift(q, r, -1)
                if not early(pq):
                    xnT_io(pq, pr)

            for r in range(RT):
                attention_io(0, r)
                if r > 0:
                    weights(0, r - 1)
            with sp.Fori(1, B - 1) as b:
                for r in range(RT):
                    attention_io(b, r)
                    if r > 0:
                        weights(b, r - 1)
            def shared_load(q, r):
                n = num(q, r)
                if isinstance(q, int) and q == 0:
                    sp.wait_ge(st_x2[r], 16 * B)
                else:
                    sp.wait_ge(y_s, n - SLOTS + 1)
                    sp.wait_ge(xlo_s, n - SLOTS + 1)
                sp.wait_ge(st_xnT[r % 2], stored_xnT(q, r))
                sp.wait_ge(st_xn[r], 16 * B)
                sp.dma_start(xg[:, r, :], xnT_t[n]).then_inc(ld_xg[r], 16)
                sp.dma_start(x2[:, r, :], out_t[n]).then_inc(ld_x2[r], 16)

            def shared_store(q, r):
                n = num(q, r)
                sp.wait_ge(y_s, n + 1)
                sp.dma_start(out_t[n], y[:, r, :]).then_inc(st_y[r], 16)

            for r in range(RT):
                attention_io(B - 1, r, last=True)
            shared_load(0, 0)
            xnT_io(B - 1, RT - 1)
            for r in range(1, SLOTS):
                shared_load(0, r)
            for i in range(3):
                weights(B - 1, i)
            for n in range(TILES):
                q, r = n // SLOTS, n % SLOTS
                if n == MAP_JOB - 1:
                    sp.wait_ge(map_ps, 1)
                    for i in range(3):
                        weights(B + 1, i)
                if n >= MAP_JOB:
                    for c in late_chunks(n):
                        if c + 3 < 3 * LN:
                            weights(B + 1 + (c + 3) // 3, c % 3)
                shared_store(q, r)
                if q + 1 < J0:
                    shared_load(q + 1, r)
                if n < 3:
                    weights(B, n)

        @block.gpsimd
        def _(pool):
            steps = [0]

            def then(ins):
                steps[0] += 1
                ins.then_inc(pool_step, 1)
                pool.wait_ge(pool_step, steps[0])

            g = nc.gpsimd
            then(g.memset(ident[:], 0.0))
            then(g.affine_select(out=ident[:], in_=ident[:], compare_op=ALU.not_equal, fill=1.0, base=0,
                                 pattern=[[-1, P]], channel_multiplier=1))
            g.memset(ones[:], 1.0)
            g.memset(jprob[:, 0:TILES], 1.0)
            g.memset(jexpert[:, 0:TILES], SHARED)
            g.memset(mhalf[:], -0.5).then_inc(c_pool, 1)
            zeros = xT[:].rearrange("p s k t -> p (s k t)")[:, 0:D]
            then(g.memset(zeros, 0.0))
            g.dma_start(out_t[TILES], zeros).then_inc(st_trash, 16)
            pool.wait_ge(pen_ready0, 2)

            def penalty(q, r):
                if not (isinstance(q, int) and q == 0):
                    pool.wait_ge(max_s, before(pool, num(q, r) - SLOTS + 1))
                g.tensor_tensor(pen[:, r, :], mask_pen[:, r, :], kpad_pen[:, q, :], ALU.add).then_inc(pen_s, 1)

            def inv_std(q, r, stat_s, mv, ve, ve_s, rstd, rstd_s):
                t = num(q, r)
                pool.wait_ge(stat_s, before(pool, t + 1))
                g.tensor_scalar(ve[:, r:r + 1], mv[:, r, 1:2], EPS, None, ALU.add).then_inc(ve_s, 1)
                pool.wait_ge(ve_s, before(pool, t + 1))
                g.tensor_tensor(rstd[:, r:r + 1], ve[:, r:r + 1], mhalf[:], ALU.pow).then_inc(rstd_s, 1)

            def low_part(place, i, c):
                pool.wait_ge(hi_s, before(pool, c + 1))
                g.tensor_tensor(third((gu_lo, dn_lo), place, i), stage[:, i],
                                third((gu_hi, dn_hi), place, i).bitcast(f32), ALU.subtract).then_inc(lo_s, 1)

            def step(q, r):
                fixed = isinstance(q, int)
                if not (fixed and num(q, r) + 1 >= TILES):
                    nq, nr = shift(q, r, 1)
                    inv_std(nq, nr, xstat, mv1, ve1, ve1_s, rstd1, rstd1_s)
                if not (fixed and num(q, r) == 0):
                    pq, pr = shift(q, r, -1)
                    inv_std(pq, pr, mv2_s, mv2, ve2, ve2_s, rstd2, rstd2_s)
                if fixed and num(q, r) == TILES - 1:
                    inv_std(q, r, mv2_s, mv2, ve2, ve2_s, rstd2, rstd2_s)
                if r > 0:
                    low_part(q, r - 1, chunk_number(q - 1, r - 1))
                if not (fixed and num(q, r) + 2 >= TILES):
                    penalty(*shift(q, r, 2))

            inv_std(0, 0, xstat, mv1, ve1, ve1_s, rstd1, rstd1_s)
            penalty(0, 0)
            penalty(0, 1)
            for r in range(RT):
                step(0, r)
            with pool.Fori(1, B - 1) as b:
                for r in range(RT):
                    step(b, r)
            for r in range(RT):
                step(B - 1, r)

            def iota(dst, pattern, base_, mult):
                return g.iota(dst, pattern=pattern, base=base_, channel_multiplier=mult,
                              allow_small_or_imprecise_dtypes=True)
            pool.wait_ge(max_s, TILES)
            iota(idx8, [[0, TILES], [-1, E]], E, 0).then_inc(first_table, 1)
            iota(k128, [[0, E], [P, TILES]], 0, 0)
            iota(a128[:], [[P, NG]], 1, 0)
            iota(tok1[:], [[0, K], [P, TILES]], 1, 1)
            iota(iota1[:], [[1, P]], 1, 0)
            iota(pidx[:], [[0, 1]], T + 1, 1)
            then(g.memset(triangle[:], 1.0))
            g.affine_select(out=triangle[:], in_=triangle[:], compare_op=ALU.is_gt, fill=0.0, base=0,
                            pattern=[[1, P]], channel_multiplier=-1).then_inc(consts_s, 1)

            for c in range(6):
                low_part(B + c // 3, c % 3, chunk_number(B - 1, c))

            pool.wait_ge(G_s, 1)
            pool.wait_ge(prob_s, 1)
            pool.wait_ge(lo_s, chunk_number(B, 2) + 1)
            then(g.tensor_tensor(R[:, :, 0], G[:, :, 0:ROUTED], G[:, :, 1:NG], ALU.subtract))
            then(g.tensor_tensor(R[:, :, 1], R[:, :, 0],
                                 prob[:].rearrange("p k t -> p (k t)").unsqueeze(2).to_broadcast([P, K * TILES, ROUTED]),
                                 ALU.mult))
            g.tensor_tensor(R[:, :, 0], R[:, :, 0],
                            tok1[:].rearrange("p k t -> p (k t)").unsqueeze(2).to_broadcast([P, K * TILES, ROUTED]),
                            ALU.mult).then_inc(R_s, 1)

            def gather(q, r):
                n = num(q, r)
                if isinstance(q, int) and q == J0:
                    pool.wait_ge(table_s, 1)
                    pool.wait_ge(xlo_s, n - SLOTS + 1)
                else:
                    pool.wait_ge(jxT_ps, before(pool, n - TILES - SLOTS + 1))
                g.tensor_copy(gidx[:, r, :], jgather[:, bass.ds(n - TILES, 1)]).then_inc(gidx_s, 1)
                pool.wait_ge(gidx_s, before(pool, n - TILES + 1))
                g.indirect_dma_start(
                    out=xg[:, r, :], out_offset=None, in_=xn_dram,
                    in_offset=bass.IndirectOffsetOnAxis(ap=gidx[:, r, :], axis=0),
                    bounds_check=T - 1).then_inc(gt_xg[r], 16)

            def scatter(q, r, after_scatter=True):
                n = num(q, r)
                g.tensor_copy(sidx[:, r, :], jscatter[:, bass.ds(n - TILES, 1)]).then_inc(sidx_s, 1)
                pool.wait_ge(sidx_s, before(pool, n - TILES + 1))
                pool.wait_ge(y_s, before(pool, n + 1))
                if after_scatter:
                    pq, pr = shift(q, r, -1)
                    pool.wait_ge(add_y[pr], before(pool, 16 * (pq - J0 + 1)))
                g.indirect_dma_start(
                    out=out, out_offset=bass.IndirectOffsetOnAxis(ap=sidx[:, r, :], axis=0),
                    in_=y[:, r, :], in_offset=None, bounds_check=T + P - 1, compute_op=ALU.add).then_inc(add_y[r], 16)

            for n in range(MAP_JOB, TILES):
                if n > MAP_JOB + 1:
                    gather(J0, n - MAP_JOB - 2)
                for c in late_chunks(n):
                    if c % 3 < 2:
                        low_part(B + 2 + c // 3, c % 3, chunk_number(B + 1, c))
            for r in range(SLOTS):
                pool.wait_ge(st_y[r], 16 * J0)
            pool.wait_ge(st_trash, 16)
            QL = ROUTED // SLOTS
            for r in range(SLOTS):
                scatter(J0, r, after_scatter=(r > 0))
                gather(J0 + 1, r)
            with pool.Fori(J0 + 1, J0 + QL - 1) as q:
                for r in range(SLOTS):
                    scatter(q, r)
                    gather(q + 1, r)
            for r in range(SLOTS):
                scatter(J0 + QL - 1, r)
                if r < ROUTED % SLOTS:
                    gather(J0 + QL, r)
            for r in range(ROUTED % SLOTS):
                scatter(J0 + QL, r)
            for r in range(SLOTS):
                pool.wait_ge(add_y[r], 16 * (QL + (1 if r < ROUTED % SLOTS else 0)))

        @block.scalar
        def _(act):
            a = nc.scalar
            act.dma_start(mask_in[:], mask.rearrange("(r p) s -> p r s", p=P)).then_inc(ld_mask, 16)
            act.dma_start(kpad_in[:].rearrange("p b s -> p (b s)"),
                          kpad.rearrange("b s -> (b s)").partition_broadcast(P)).then_inc(ld_mask, 16)
            act.wait_ge(ld_small, 64)
            a.mul(bqk[:, 0:1], bqk[:, 0:1], SCALING).then_inc(bq_ready, 1)
            act.wait_ge(wT_ps, 1)
            a.copy(wqkT[:].rearrange("p w o -> p (w o)"), ps_proj[0][:, 0:2 * H]).then_inc(wT_ready, 1)
            act.wait_ge(bq_ready, 1)

            def ctx_copy(b):
                act.wait_ge(ctxT_ps, b + 1)
                if b >= 2:
                    act.wait_ge(proj_ps, 2 * (b - 1))
                a.copy(ctxT[:, b % 2, :], ps_ctxT[:]).then_inc(ctxT_ready, 1)

            def projections(b):
                for w, dst in enumerate((qT, kT)):
                    act.wait_ge(proj_ps, 2 * b + w + 1)
                    a.activation(dst[:, b * S:(b + 1) * S], ps_proj[w][:], ACT.Identity, bias=bqk[:, w:w + 1],
                                 scale=SCALING if w == 0 else 1.0).then_inc(proj_ready, 1)

            def q_copy(q, r):
                t = num(q, r)
                if not (isinstance(q, int) and q == 0):
                    act.wait_ge(score_ps, t - SLOTS + 1)
                a.copy(q_tile[:, r, :], qT[:, bass.ds(P * t, P)]).then_inc(q_ready, 1)

            def expo(q, r):
                t = num(q, r)
                act.wait_ge(nbias_s, t + 1)
                a.activation(sc[:, r, :], sc[:, r, :], ACT.Exp, bias=nbias[:, r:r + 1], scale=rstd1[:, r:r + 1],
                             accum_out=rowsum[:, r:r + 1]).then_inc(exp_s, 1)

            def xnT_copy(q, r):
                t = num(q, r)
                act.wait_ge(xnT_ps, t + 1)
                if not (isinstance(q, int) and t < 2):
                    act.wait_ge(st_xnT[r % 2], stored_xnT(*shift(q, r, -2)))
                a.copy(xT[:, r % 2].rearrange("p k t -> p (k t)"), ps_xnT[r % 2][:]).then_inc(xnT_ready, 1)

            def high_part(place, i, c, visit):
                act.wait_ge(ld_st[i], 32 * (visit + 1))
                a.copy(third((gu_hi, dn_hi), place, i), stage[:, i]).then_inc(hi_s, 1)

            def step(q, r, drop_q=False, project=None):
                expo(q, r)
                if project is not None:
                    projections(project)
                if not drop_q:
                    q_copy(*shift(q, r, 2))
                if project is not None and project + 1 < B:
                    ctx_copy(project + 1)
                if r < 3:
                    high_part(q, r, chunk_number(q - 1, r), q)
                tq, tr = shift(q, r, -2)
                if not early(tq):
                    xnT_copy(tq, tr)

            ctx_copy(0)
            projections(0)
            act.wait_ge(st_trash, 16)
            act.wait_ge(proj_ready, 2)
            q_copy(0, 0)
            q_copy(0, 1)
            ctx_copy(1)
            for t in range(HEAD):
                if t in (2, 3):
                    act.wait_ge(proj_ready, 4 if t == 2 else 2 * B)
                step(t // RT, t % RT, project=t + 1 if t + 1 < B else None)
            with act.Fori(1, LOOP_END) as b:
                for d in range(RT):
                    step(*shift(b, LAG, d))
            for t in range(TILES - LAG, TILES):
                step(t // RT, t % RT, drop_q=True)
            xnT_copy(B - 1, RT - 2)
            xnT_copy(B - 1, RT - 1)
            act.wait_ge(logit_ps, TILES)
            a.copy(lg[:].rearrange("p t e -> p (t e)"), ps_logit[:, 0:TILES * E]).then_inc(lg_s, 1)

            def x_high(q, r):
                n = num(q, r)
                if is_shared(q):
                    act.wait_ge(ld_xg[r], 16 * (q + 1))
                else:
                    act.wait_ge(jxT_ps, n - TILES + 1)
                if not (isinstance(q, int) and n < 2):
                    act.wait_ge(g_ps, n - 1)
                a.copy(x_hi[:, r % 2], rows_T(q, r)).then_inc(xhi_s, 1)
                a.copy(x_bf[:, r % 2], rows_T(q, r)).then_inc(xbf_s, 1)

            def h_high(q, r):
                n = num(q, r)
                act.wait_ge(hT_ps, n + 1)
                if not (isinstance(q, int) and n < 2):
                    act.wait_ge(y_ps, n - 1)
                bank_ = ps_hT[:, 0:I].rearrange("p (c t) -> p c t", c=IC)
                a.copy(h_hi[:, r % 2], bank_).then_inc(hhi_s, 1)
                a.copy(h_bf[:, r % 2], bank_).then_inc(hbf_s, 1)

            def silu(q, r):
                n = num(q, r)
                act.wait_ge(g_ps, n + 1)
                if not (isinstance(q, int) and n < 2):
                    act.wait_ge(hT_ps, n - 1)
                a.activation(h[:, r % 2, :], ps_g[r % 2][:, 0:I], ACT.Silu,
                             scale=jprob[:, bass.ds(n, 1)]).then_inc(silu_s, 1)

            def job_step(q, r, last=False):
                pq, pr = shift(q, r, -1)
                if not early(pq):
                    h_high(pq, pr)
                silu(q, r)
                if not last:
                    x_high(*shift(q, r, 1))

            for r in range(SLOTS):
                act.wait_ge(st_xn[r], 16 * B)
            for p in range(2):
                act.wait_ge(st_xnT[p], 16 * TILES // 2)
            act.wait_ge(logit_ps, TILES)
            x_high(0, 0)
            act.wait_ge(top_s, 1)
            a.activation(pexp[:], top[:], ACT.Exp, scale=-1.0).then_inc(pexp_s, 1)
            for n in range(MAP_JOB):
                if n == 2:
                    act.wait_ge(rank_ps, 1)
                    a.copy(rank.rearrange("p a t e -> p (a t e)"), ps_rank[:, 0:2 * TILES * E]).then_inc(rank_s, 1)
                job_step(n // SLOTS, n % SLOTS)
                if n < 6:
                    high_part(B + n // 3, n % 3, chunk_number(B - 1, n), B + n // 3)
            act.wait_ge(map_ps, 1)
            a.copy(amap[:].rearrange("p a j -> p (a j)"), ps_map[:, 0:2 * ROUTED]).then_inc(map_s, 1)
            for n in range(MAP_JOB, TILES):
                if n == TILES - 1:
                    act.wait_ge(table_s, 1)
                job_step(n // SLOTS, n % SLOTS)
                for c in late_chunks(n):
                    e, i = B + 1 + c // 3, c % 3
                    high_part(e + 1, i, chunk_number(e, i), e + 1)
            QF = JOBS // SLOTS
            with act.Fori(J0, QF) as q:
                for r in range(SLOTS):
                    job_step(q, r)
            for r in range(JOBS % SLOTS):
                job_step(QF, r, last=(r == JOBS % SLOTS - 1))
            h_high(QF, JOBS % SLOTS - 1)

        @block.vector
        def _(dve):
            v = nc.vector

            def x_stats(q, r):
                dve.wait_ge(ld_x[r], 16 * (q + 1))
                v.bn_stats(bn1[:, r, :], xin[:, r, :]).then_inc(bn1_s, 1)

            def x2_stats(q, r):
                dve.wait_ge(x2_s, num(q, r) + 1)
                v.bn_stats(bn2[:, r, :], x2[:, r, :]).then_inc(bn2_s, 1)

            def aggregate(q, r, bn, bn_s, mv, mv_s):
                dve.wait_ge(bn_s, before(dve, num(q, r) + 1))
                v.bn_aggr(mv[:, r, :], bn[:, r, :]).then_inc(mv_s, 1)

            def raw_scores(q, r):
                t = num(q, r)
                dve.wait_ge(score_ps, t + 1)
                dve.wait_ge(xstat, t + 1)
                v.scalar_tensor_tensor(sc[:, r, :], xin[:, r, :], mv1[:, r, 0:1], ps_score[r % 2][:],
                                       ALU.subtract, ALU.mult).then_inc(raw_s, 1)

            def mask_and_max(q, r):
                t = num(q, r)
                dve.wait_ge(raw_s, before(dve, t + 1))
                dve.wait_ge(pen_s, before(dve, t + 1))
                v.tensor_tensor_reduce(out=sc[:, r, :], in0=sc[:, r, :], in1=pen[:, r, :], scale=1.0, scalar=-BIG,
                                       op0=ALU.add, op1=ALU.max, accum_out=rowmax[:, r:r + 1]).then_inc(max_s, 1)

            def neg_max(q, r):
                t = num(q, r)
                dve.wait_ge(max_s, t + 1)
                dve.wait_ge(rstd1_s, t + 1)
                v.scalar_tensor_tensor(nbias[:, r:r + 1], rowmax[:, r:r + 1], -1.0, rstd1[:, r:r + 1],
                                       ALU.mult, ALU.mult).then_inc(nbias_s, 1)

            def kept_sum(q, r):
                dve.wait_ge(exp_s, num(q, r) + 1)
                v.scalar_tensor_tensor(rowsum[:, r:r + 1], rowmax[:, r:r + 1], MASKED / 2, rowsum[:, r:r + 1],
                                       ALU.is_gt, ALU.mult).then_inc(rsum_s, 1)

            def inv_sum(q, r):
                dve.wait_ge(rsum_s, num(q, r) + 1)
                v.reciprocal(rinv[:, r:r + 1], rowsum[:, r:r + 1]).then_inc(rinv_s, 1)

            def residual(q, r):
                dve.wait_ge(rinv_s, num(q, r) + 1)
                if not (isinstance(q, int) and q == 0):
                    dve.wait_ge(st_x2[r], 16 * q)
                v.scalar_tensor_tensor(x2[:, r, :], sc[:, r, :], rinv[:, r:r + 1], xin[:, r, :],
                                       ALU.mult, ALU.add).then_inc(x2_s, 1)

            def normal(q, r):
                t = num(q, r)
                dve.wait_ge(rstd2_s, t + 1)
                if not (isinstance(q, int) and q == 0):
                    dve.wait_ge(st_xn[r], 16 * q)
                    dve.wait_ge(xnT_ps, t - SLOTS + 1)
                v.tensor_scalar(xn[:, r, :], x2[:, r, :], mv2[:, r, 0:1], rstd2[:, r:r + 1],
                                ALU.subtract, ALU.mult).then_inc(xn_s, 1)

            def step(q, r, last=False):
                one, two = shift(q, r, -1), shift(q, r, -2)
                lag1, lag2 = not early(one[0]), not early(two[0])
                raw_scores(q, r)
                if lag1:
                    kept_sum(*one)
                    inv_sum(*one)
                    residual(*one)
                mask_and_max(q, r)
                neg_max(q, r)
                if not last:
                    x_stats(*shift(q, r, 1))
                if lag1:
                    x2_stats(*one)
                if not last:
                    aggregate(*shift(q, r, 1), bn1, bn1_s, mv1, xstat)
                if lag2:
                    normal(*two)
                if lag1:
                    aggregate(*one, bn2, bn2_s, mv2, mv2_s)

            dve.wait_ge(ld_mask, 32)
            v.tensor_scalar(mask_pen, mask_in[:], MASKED, None, ALU.mult).then_inc(pen_ready0, 1)
            v.tensor_scalar(kpad_pen, kpad_in[:], MASKED, None, ALU.mult).then_inc(pen_ready0, 1)
            x_stats(0, 0)
            aggregate(0, 0, bn1, bn1_s, mv1, xstat)
            for t in range(HEAD):
                step(t // RT, t % RT)
            with dve.Fori(1, LOOP_END) as b:
                for d in range(RT):
                    step(*shift(b, LAG, d))
            for t in range(TILES - LAG, TILES):
                step(t // RT, t % RT, last=(t == TILES - 1))
            kept_sum(B - 1, RT - 1)
            inv_sum(B - 1, RT - 1)
            residual(B - 1, RT - 1)
            normal(B - 1, RT - 2)
            x2_stats(B - 1, RT - 1)
            aggregate(B - 1, RT - 1, bn2, bn2_s, mv2, mv2_s)
            normal(B - 1, RT - 1)

            steps = [0]

            def then(ins):
                steps[0] += 1
                ins.then_inc(dve_step, 1)
                dve.wait_ge(dve_step, steps[0])

            def wide(column, shape):
                return column.unsqueeze(2).to_broadcast(shape)

            def choose():
                dve.wait_ge(first_table, 1)
                dve.wait_ge(lg_s, 1)
                src = lg[:]
                for k in range(K):
                    then(v.tensor_reduce(top[:, k], src, X, ALU.max))
                    then(v.tensor_tensor(eq, src, wide(top[:, k], [P, TILES, E]), ALU.is_equal))
                    then(v.tensor_tensor(eq, eq, idx8, ALU.mult))
                    then(v.tensor_reduce(best[:], eq, X, ALU.max))
                    then(v.tensor_tensor(oh[:, k], idx8, wide(best[:], [P, TILES, E]), ALU.is_equal))
                    if k == 0:
                        then(v.scalar_tensor_tensor(lg2, oh[:, 0], -BIG, lg[:], ALU.mult, ALU.add))
                        src = lg2
                v.tensor_scalar(top[:], top[:], -88.0, BIG, ALU.max, ALU.min).then_inc(top_s, 1)
                v.tensor_tensor(ohs[:], oh[:, 0], oh[:, 1], ALU.add).then_inc(oh_s, 1)

            def count():
                dve.wait_ge(consts_s, 1)
                dve.wait_ge(rank_s, 1)
                v.tensor_reduce(cnt[:], rank[:, 1].rearrange("p t e -> p e t"), X, ALU.add)
                then(v.tensor_copy(cum[:, 0], rank[:, 1]))
                then(v.tensor_tensor(cmp, wide(cnt[:], [P, E, TILES]), k128, ALU.is_gt))
                then(v.tensor_reduce(ntile[:, 0], cmp, X, ALU.add))
                for i, d in enumerate((1, 2, 4)):
                    v.tensor_copy(ntile[:, i + 1, 0:d], ntile[:, i, 0:d])
                    then(v.tensor_tensor(ntile[:, i + 1, d:], ntile[:, i, d:], ntile[:, i, 0:E - d], ALU.add))
                then(v.tensor_tensor(base[:], ntile[:, 3], ntile[:, 0], ALU.subtract))

            def weights_of_choices():
                dve.wait_ge(pexp_s, 1)
                then(v.tensor_scalar(prob[:], pexp[:], 1.0, None, ALU.add))
                v.reciprocal(prob[:], prob[:]).then_inc(prob_s, 1)

            def earlier_tiles():
                side = 0
                for d in (1, 2, 4, 8):
                    v.tensor_copy(cum[:, 1 - side, 0:d], cum[:, side, 0:d])
                    then(v.tensor_tensor(cum[:, 1 - side, d:], cum[:, side, d:], cum[:, side, 0:TILES - d], ALU.add))
                    side = 1 - side

            def places():
                then(v.tensor_tensor(place, cum[:, 0], rank[:, 1], ALU.subtract))
                then(v.tensor_scalar(base[:], base[:], float(P), 1.0, ALU.mult, ALU.add))
                then(v.tensor_tensor(place, place, rank[:, 0], ALU.add))
                then(v.tensor_tensor(place, place, base[:].unsqueeze(1).to_broadcast([P, TILES, E]), ALU.add))

            def place_of_choice():
                for k in range(K):
                    then(v.tensor_tensor(eq, oh[:, k], place, ALU.mult))
                    then(v.tensor_reduce(slot1[:, k], eq, X, ALU.add))

            slots = slot1[:].rearrange("p k t -> p (k t)")

            def job_of_choice():
                v.tensor_tensor(G, wide(slots, [P, K * TILES, NG]),
                                a128[:].unsqueeze(1).to_broadcast([P, K * TILES, NG]), ALU.is_ge).then_inc(G_s, 1)

            def job_of_choice_sum():
                dve.wait_ge(G_s, 1)
                then(v.tensor_reduce(acol[:], G[:, :, 1:NG], X, ALU.add))
                then(v.scalar_tensor_tensor(bcol[:], acol[:], -float(P), slots, ALU.mult, ALU.add))

            def row_of_choice(part):
                n = K * TILES // 4
                c0, c1 = part * n, (part + 1) * n
                v.tensor_tensor(OB[:, c0:c1], iota1[:].unsqueeze(1).to_broadcast([P, n, P]),
                                wide(bcol[:, c0:c1], [P, n, P]), ALU.is_equal).then_inc(OB_s, 1)

            def job_experts():
                then(v.tensor_scalar(ntile[:, 0], ntile[:, 3], float(P), 1.0, ALU.mult, ALU.add))
                then(v.tensor_tensor(ecmp[:], wide(a128[:, 0:ROUTED], [P, ROUTED, E]),
                                     ntile[:, 0].unsqueeze(1).to_broadcast([P, ROUTED, E]), ALU.is_ge))
                then(v.tensor_reduce(efl[:], ecmp[:], X, ALU.add))
                v.tensor_scalar(jexpert[:, TILES:JOBS], efl[:], float(E - 1), 1.0, ALU.min, ALU.add)

            def tables():
                dve.wait_ge(map_s, 1)
                then(v.tensor_scalar(hole[:], amap[:, 0], 0.0, None, ALU.is_equal))
                v.tensor_scalar(jgather[:], amap[:, 0], -1.0, 0.0, ALU.add, ALU.max)
                then(v.scalar_tensor_tensor(jf[:], hole[:], pidx[:], amap[:, 0], ALU.mult, ALU.add))
                v.tensor_copy(jprob[:, TILES:JOBS], amap[:, 1])
                v.tensor_scalar(jscatter[:], jf[:], -1.0, None, ALU.add).then_inc(table_s, 1)

            def h_low(q, r):
                n = num(q, r)
                dve.wait_ge(hbf_s, n + 1)
                if not (isinstance(q, int) and n < 2):
                    dve.wait_ge(y_ps, n - 1)
                v.tensor_tensor(h_lo[:, r % 2], ps_hT[:, 0:I].rearrange("p (c t) -> p c t", c=IC),
                                h_hi[:, r % 2].bitcast(f32), ALU.subtract).then_inc(hlo_s, 1)

            def x_low(q, r):
                n = num(q, r)
                dve.wait_ge(xbf_s, n + 1)
                if not (isinstance(q, int) and n < 2):
                    dve.wait_ge(g_ps, n - 1)
                v.tensor_tensor(x_lo[:, r % 2], rows_T(q, r),
                                x_hi[:, r % 2].bitcast(f32), ALU.subtract).then_inc(xlo_s, 1)

            def down_low_part(expert):
                dve.wait_ge(hi_s, chunk_number(expert, 2) + 1)
                v.tensor_tensor(dn_lo[:, expert + 1], stage[:, 2], dn_hi[:, expert + 1].bitcast(f32),
                                ALU.subtract).then_inc(down_lo_s, 1)

            def gated(q, r):
                n = num(q, r)
                if isinstance(q, int) and n == TILES:
                    dve.wait_ge(table_s, 1)
                dve.wait_ge(silu_s, n + 1)
                v.scalar_tensor_tensor(h[:, r % 2, :], ps_g[r % 2][:, I:2 * I], jprob[:, bass.ds(n, 1)],
                                       h[:, r % 2, :], ALU.mult, ALU.mult).then_inc(h_s, 1)

            def y_out(q, r, shared):
                n = num(q, r)
                dve.wait_ge(y_ps, n + 1)
                if isinstance(q, int) and 0 < q <= J0:
                    dve.wait_ge(st_y[r], 16 * q)
                elif not isinstance(q, int) or q > J0:
                    dve.wait_ge(add_y[r], 16 * (q - J0))
                if shared:
                    dve.wait_ge(ld_x2[r], 16 * (q + 1))
                    v.tensor_tensor(y[:, r, :], ps_y[r % 2][:], x2[:, r, :], ALU.add).then_inc(y_s, 1)
                else:
                    v.tensor_copy(y[:, r, :], ps_y[r % 2][:]).then_inc(y_s, 1)

            def job_step(q, r, shared=False, last=False):
                pq, pr = shift(q, r, -1)
                if not early(pq):
                    h_low(pq, pr)
                gated(q, r)
                if not last:
                    x_low(*shift(q, r, 1))
                if not early(pq):
                    y_out(pq, pr, shared)

            for r in range(SLOTS):
                dve.wait_ge(st_xn[r], 16 * B)
            choose()
            x_low(0, 0)
            pieces = {2: [count], 3: [earlier_tiles], 4: [places, weights_of_choices], 5: [place_of_choice],
                      6: [job_of_choice], 7: [job_of_choice_sum, lambda: row_of_choice(0)],
                      8: [lambda: row_of_choice(1)],
                      9: [lambda: row_of_choice(2), lambda: row_of_choice(3), job_experts], MAP_JOB: [tables]}
            for n in range(TILES + 1):
                if n > MAP_JOB:
                    for c in late_chunks(n - 1):
                        if c % 3 == 2:
                            down_low_part(B + 1 + c // 3)
                job_step(n // SLOTS, n % SLOTS, shared=True)
                for piece in pieces.get(n, []):
                    piece()
            QF = JOBS // SLOTS
            for r in range(1, SLOTS):
                job_step(J0, r)
            with dve.Fori(J0 + 1, QF) as q:
                for r in range(SLOTS):
                    job_step(q, r)
            for r in range(JOBS % SLOTS):
                job_step(QF, r, last=(r == JOBS % SLOTS - 1))
            lq, lr = QF, JOBS % SLOTS - 1
            h_low(lq, lr)
            y_out(lq, lr, False)

        @block.tensor
        def _(pe):
            tn = nc.tensor
            pe.wait_ge(c_pool, 1)
            pe.wait_ge(ld_small, 64)
            for w in range(2):
                last = tn.transpose(ps_proj[0][:, w * H:(w + 1) * H], wqk[:, w, :], ident[:])
            last.then_inc(wT_ps, 1)

            def ctx_transpose(b):
                pe.wait_ge(ld_ctx if b else ld_ctx0, 16)
                if b:
                    pe.wait_ge(ctxT_ready, b)
                for r in range(RT):
                    last = tn.transpose(ps_ctxT[:, r * P:(r + 1) * P], ctx_in[:, b * RT + r, :], ident[:])
                last.then_inc(ctxT_ps, 1)

            def projections(b):
                if b == 0:
                    pe.wait_ge(wT_ready, 1)
                pe.wait_ge(ctxT_ready, b + 1)
                for w in range(2):
                    if b:
                        pe.wait_ge(proj_ready, 2 * b - 1 + w)
                    tn.matmul(ps_proj[w][:], wqkT[:, w, :], ctxT[:, b % 2, :], start=True, stop=True).then_inc(proj_ps, 1)

            def scores(q, r):
                t = num(q, r)
                pe.wait_ge(q_ready, t + 1)
                if not (isinstance(q, int) and num(q, r) < 2):
                    pe.wait_ge(raw_s, t - 1)
                tn.matmul(ps_score[r % 2][:], q_tile[:, r, :], kT[:, bass.ds(S * q, S)], start=True,
                          stop=True).then_inc(score_ps, 1)

            def xn_transpose(q, r):
                t = num(q, r)
                pe.wait_ge(xn_s, t + 1)
                if not (isinstance(q, int) and num(q, r) < 2):
                    pe.wait_ge(xnT_ready, t - 1)
                for k in range(KC):
                    last = tn.transpose(ps_xnT[r % 2][:, k * P:(k + 1) * P], xn[:, r, k * P:(k + 1) * P], ident[:])
                last.then_inc(xnT_ps, 1)

            def logits(q, r):
                t = num(q, r)
                pe.wait_ge(xnT_ready, t + 1)
                for k in range(KC):
                    last = tn.matmul(ps_logit[:, bass.ds(E * t, E)], xT[:, r % 2, k, :], rw[:, k, :],
                                     start=(k == 0), stop=(k == KC - 1))
                last.then_inc(logit_ps, 1)

            def step(q, r, last=False, project=None):
                if project is not None:
                    projections(project)
                if not last:
                    scores(*shift(q, r, 2))
                if project is not None and project + 1 < B:
                    ctx_transpose(project + 1)
                pq, pr = shift(q, r, -2)
                if not early(pq):
                    xn_transpose(pq, pr)
                pq, pr = shift(q, r, -3)
                if not early(pq):
                    logits(pq, pr)

            ctx_transpose(0)
            projections(0)
            ctx_transpose(1)
            pe.wait_ge(proj_ready, 2)
            scores(0, 0)
            scores(0, 1)
            pe.wait_ge(ld_rw, 16)
            for t in range(HEAD):
                if t in (2, 3):
                    pe.wait_ge(proj_ready, 4 if t == 2 else 2 * B)
                step(t // RT, t % RT, project=t + 1 if t + 1 < B else None)
            with pe.Fori(1, LOOP_END) as b:
                for d in range(RT):
                    step(*shift(b, LAG, d))
            for t in range(TILES - LAG, TILES):
                step(t // RT, t % RT, last=True)
            for r in (RT - 2, RT - 1):
                xn_transpose(B - 1, r)
                logits(B - 1, r - 1)

            def x_transpose(q, r):
                n = num(q, r)
                pe.wait_ge(gt_xg[r], 16 * (q - J0 + 1))
                if isinstance(q, int) and n < TILES + 2:
                    pe.wait_ge(xnT_ready, TILES)
                else:
                    pe.wait_ge(xlo_s, n - 1)
                for k in range(KC):
                    last = tn.transpose(ps_xT[r % 2][:, k * P:(k + 1) * P], xg[:, r, k * P:(k + 1) * P], ident[:])
                last.then_inc(jxT_ps, 1)

            def expert(n):
                return pe.value_load(jexpert[0:1, bass.ds(n, 1)], min_val=0, max_val=E)

            def gate_up(q, r, e):
                n = num(q, r)
                pe.wait_ge(xhi_s, n + 1)
                if not (isinstance(q, int) and num(q, r) < 2):
                    pe.wait_ge(h_s, n - 1)
                for k in range(KC):
                    tn.matmul(ps_g[r % 2][:], x_hi[:, r % 2, k, :], gu_hi[:, e, k, :], start=(k == 0), stop=False)

                def low_weights(stop):
                    pe.wait_ge(xbf_s, n + 1)
                    if r == 0 and not is_shared(q):
                        pe.wait_ge(lo_s, FIRST_LATE + 2 * LN)
                    for k in range(KC):
                        last = tn.matmul(ps_g[r % 2][:], x_bf[:, r % 2, k, :], gu_lo[:, e, k, :], start=False,
                                         stop=(stop and k == KC - 1))
                    return last

                def low_rows(stop):
                    pe.wait_ge(xlo_s, n + 1)
                    for k in range(KC):
                        last = tn.matmul(ps_g[r % 2][:], x_lo[:, r % 2, k, :], gu_hi[:, e, k, :], start=False,
                                         stop=(stop and k == KC - 1))
                    return last

                if is_shared(q):
                    low_weights(False)
                    low_rows(True).then_inc(g_ps, 1)
                else:
                    low_rows(False)
                    low_weights(True).then_inc(g_ps, 1)

            def h_transpose(q, r):
                n = num(q, r)
                pe.wait_ge(h_s, n + 1)
                if not (isinstance(q, int) and num(q, r) == 0):
                    pe.wait_ge(hlo_s, n)
                    pe.wait_ge(hbf_s, n)
                for c in range(IC):
                    last = tn.transpose(ps_hT[:, c * P:(c + 1) * P], h[:, r % 2, c * P:(c + 1) * P], ident[:])
                last.then_inc(hT_ps, 1)

            def down(q, r):
                n = num(q, r)
                e = expert(n)
                pe.wait_ge(hhi_s, n + 1)
                if not (isinstance(q, int) and num(q, r) < 2):
                    pe.wait_ge(y_s, n - 1)
                for c in range(IC):
                    tn.matmul(ps_y[r % 2][:], h_hi[:, r % 2, c, :], dn_hi[:, e, c, :], start=(c == 0), stop=False)
                pe.wait_ge(hbf_s, n + 1)
                for c in range(IC):
                    tn.matmul(ps_y[r % 2][:], h_bf[:, r % 2, c, :], dn_lo[:, e, c, :], start=False, stop=False)
                pe.wait_ge(hlo_s, n + 1)
                for c in range(IC):
                    last = tn.matmul(ps_y[r % 2][:], h_lo[:, r % 2, c, :], dn_hi[:, e, c, :], start=False,
                                     stop=(c == IC - 1))
                last.then_inc(y_ps, 1)

            def job_step(q, r, last=False):
                pq, pr = shift(q, r, -1)
                e = expert(num(q, r))
                if not early(pq):
                    h_transpose(pq, pr)
                gate_up(q, r, e)
                if not last and not is_shared(shift(q, r, 1)[0]):
                    x_transpose(*shift(q, r, 1))
                if not early(pq):
                    down(pq, pr)

            logits(B - 1, RT - 1)
            pe.wait_ge(raw_s, TILES)
            pe.wait_ge(lo_s, 3)
            job_step(0, 0)
            job_step(0, 1)
            pe.wait_ge(consts_s, 1)
            pe.wait_ge(oh_s, 1)
            tn.matmul(ps_rank[:, 0:TILES * E], triangle[:], ohs[:].rearrange("p t e -> p (t e)"), start=True, stop=True)
            tn.matmul(ps_rank[:, TILES * E:2 * TILES * E], ones[:], ohs[:].rearrange("p t e -> p (t e)"),
                      start=True, stop=True).then_inc(rank_ps, 1)
            for n in range(2, MAP_JOB):
                job_step(n // SLOTS, n % SLOTS)
            pe.wait_ge(R_s, 1)
            for i in range(K * TILES):
                if i % (K * TILES // 4) == 0:
                    pe.wait_ge(OB_s, i // (K * TILES // 4) + 1)
                last = tn.matmul(ps_map[:, 0:2 * ROUTED], OB[:, i, :], R[:, i].rearrange("p a j -> p (a j)"),
                                 start=(i == 0), stop=(i == K * TILES - 1))
            last.then_inc(map_ps, 1)
            for n in range(MAP_JOB, TILES):
                if n == TILES - 1:
                    pe.wait_ge(table_s, 1)
                job_step(n // SLOTS, n % SLOTS)
            pe.wait_ge(hi_s, FIRST_LATE + 3 * LN - 1)
            QF = JOBS // SLOTS
            with pe.Fori(TILES // SLOTS, QF) as q:
                for r in range(SLOTS):
                    if r == 1:
                        pe.wait_ge(down_lo_s, LN)
                    job_step(q, r)
            for r in range(JOBS % SLOTS):
                job_step(QF, r, last=(r == JOBS % SLOTS - 1))
            h_transpose(QF, JOBS % SLOTS - 1)
            down(QF, JOBS % SLOTS - 1)


_INS = ['x', 'ctx_512', 'mask_SxS2_bk1', 'mask_BxS2_bf0', 'L0_xattn_Wq', 'L0_xattn_bq', 'L0_xattn_Wk',
        'L0_xattn_bk', 'L0_ffn_router_w', 'L0_ffn_gate_up_w', 'L0_ffn_down_w', 'L0_ffn_shared_gate_w',
        'L0_ffn_shared_up_w', 'L0_ffn_shared_down_w']


def kernel(**inputs):
    import concourse.bacc as _bacc
    from concourse.bass_utils import run_bass_kernel_spmd as _run

    nc = _bacc.Bacc("TRN2", target_bir_lowering=False, num_devices=1, dynamic_dma_scratch_size=SCRATCH)
    arrays, args = {}, []
    for name in _INS:
        a = np.ascontiguousarray(inputs[name])
        arrays[f"in_{name}"] = a
        args.append(nc.dram_tensor(f"in_{name}", a.shape, mybir.dt.from_np(a.dtype), kind="ExternalInput").ap())
    args.append(nc.dram_tensor("out_rows", (T + P, D), mybir.dt.float32, kind="ExternalOutput").ap())
    build(nc, *args)
    r = _run(nc, [arrays], core_ids=[0])
    return r.results[0]["out_rows"][:T].reshape(B, S, D)
```
